# Optimizing a Trainium2 kernel written in Bass

```python
import numpy as np
import jax
import jax.numpy as jnp

def _softmax(x, axis=-1):
    return jax.nn.softmax(x, axis=axis)

def _gelu(x):
    return jax.nn.gelu(x, approximate=True)

def _silu(x):
    return jax.nn.silu(x)

def _sigmoid(x):
    return jax.nn.sigmoid(x)

def _layernorm(x, axis=-1, eps=1e-05):
    m = jnp.mean(x, axis=axis, keepdims=True)
    v = jnp.var(x, axis=axis, keepdims=True)
    return (x - m) / jnp.sqrt(v + eps)

def _scatter_add(tgt, idx, src, axis=0):
    return tgt.at[idx].add(src)

def _segment_sum(src, seg, n):
    return jax.ops.segment_sum(src, seg, n)
kernel_name = 'mk_conv_seq_d2_conv_nchw1024_r4_e644af'

def setup_inputs(seed: int=0):
    np.random.seed(seed)
    _w = jnp.asarray

    def _rec_inputs():
        import jax
        import jax.numpy as jnp
        _gk = jax.random.key(seed)
        x = -0.0003929 + 0.9999 * jax.random.normal(jax.random.fold_in(_gk, 1), (4, 256, 16, 16), jnp.float32)
        return x
    x = _rec_inputs()

    def _L0_conv_setup():
        import jax, jax.numpy as jnp
        import numpy as np

        def conv(x, w, stride=1, pad=0):
            return jax.lax.conv_general_dilated(x, w, (stride, stride), [(pad, pad), (pad, pad)], dimension_numbers=('NCHW', 'OIHW', 'NCHW'))

        def group_norm(x, scale, bias, groups=32, eps=1e-05):
            B, C, H, W = x.shape
            xg = x.reshape(B, groups, C // groups, H, W)
            m = xg.mean(axis=(2, 3, 4), keepdims=True)
            v = xg.var(axis=(2, 3, 4), keepdims=True)
            xn = ((xg - m) * jax.lax.rsqrt(v + eps)).reshape(B, C, H, W)
            return xn * scale[None, :, None, None] + bias[None, :, None, None]

        def bilinear_sample(x, py, px):
            B, C, H, W = x.shape
            y0 = jnp.floor(py)
            x0 = jnp.floor(px)
            wy1 = py - y0
            wx1 = px - x0
            xf = x.reshape(B, C, H * W)
            Ksp = py.shape[1:]

            def corner(yi, xi, wy, wx):
                valid = (yi >= 0) & (yi < H) & (xi >= 0) & (xi < W)
                yc = jnp.clip(yi, 0, H - 1).astype(jnp.int32)
                xc = jnp.clip(xi, 0, W - 1).astype(jnp.int32)
                idx = (yc * W + xc).reshape(B, 1, -1)
                v = jnp.take_along_axis(xf, idx, axis=2).reshape(B, C, *Ksp)
                w = (wy * wx * valid).astype(x.dtype)[:, None]
                return v * w
            return corner(y0, x0, 1.0 - wy1, 1.0 - wx1) + corner(y0, x0 + 1, 1.0 - wy1, wx1) + corner(y0 + 1, x0, wy1, 1.0 - wx1) + corner(y0 + 1, x0 + 1, wy1, wx1)
        key = jax.random.key(seed)
        ks = jax.random.split(key, 8)
        B, Cin, H, W = (4, 256, 16, 16)
        Cb = 64
        x = jax.random.normal(ks[0], (B, Cin, H, W), dtype=jnp.float32)
        w1 = jax.random.normal(ks[1], (Cb, Cin, 1, 1), dtype=jnp.float32) * (1.0 / np.sqrt(Cin))
        w_off = jax.random.normal(ks[2], (27, Cb, 3, 3), dtype=jnp.float32) * 0.01
        b_off = jnp.zeros((27,), dtype=jnp.float32)
        w2 = jax.random.normal(ks[3], (Cb, Cb, 3, 3), dtype=jnp.float32) * (1.0 / np.sqrt(Cb * 9))
        w3 = jax.random.normal(ks[4], (Cin, Cb, 1, 1), dtype=jnp.float32) * (1.0 / np.sqrt(Cb))
        return {'x': x, 'w1': w1, 'gn1_scale': jnp.ones((Cb,), jnp.float32), 'gn1_bias': jnp.zeros((Cb,), jnp.float32), 'w_off': w_off, 'b_off': b_off, 'w2': w2, 'gn2_scale': jnp.ones((Cb,), jnp.float32), 'gn2_bias': jnp.zeros((Cb,), jnp.float32), 'w3': w3, 'gn3_scale': jnp.ones((Cin,), jnp.float32), 'gn3_bias': jnp.zeros((Cin,), jnp.float32), 'stride': 4}
    _L0_conv_all = _L0_conv_setup()
    _L0_conv_in = {k: v for k, v in _L0_conv_all.items() if k in ('w1', 'gn1_scale', 'gn1_bias', 'w_off', 'b_off', 'w2', 'gn2_scale', 'gn2_bias', 'w3', 'gn3_scale', 'gn3_bias')}
    del _L0_conv_all

    def _L1_conv_setup():
        import jax, jax.numpy as jnp
        import numpy as np
        WEIGHT_BITS = 5
        QUANT_BITS = 16
        BN_EPS = 1e-05

        def _quant_weight_pow2(w):
            shift_min = -(2 ** (WEIGHT_BITS - 1) - 2)
            sign = jnp.sign(w)
            p = jnp.clip(jnp.round(jnp.log2(jnp.abs(w) + 1e-20)), shift_min, 0.0)
            wq = sign * jnp.exp2(p)
            return w + jax.lax.stop_gradient(wq - w)

        def _quant_act(x):
            qmax = 2.0 ** (QUANT_BITS - 1) - 1.0
            scale = jnp.maximum(jnp.max(jnp.abs(x)), 1e-12) / qmax
            xq = jnp.round(x / scale) * scale
            return x + jax.lax.stop_gradient(xq - x)

        def _conv(x, w, stride=1, pad=0, groups=1):
            return jax.lax.conv_general_dilated(x, w, (stride, stride), [(pad, pad), (pad, pad)], dimension_numbers=('NCHW', 'OIHW', 'NCHW'), feature_group_count=groups)

        def _shift_conv(x, w, stride=1, pad=0, groups=1, bias=None):
            y = _conv(_quant_act(x), _quant_weight_pow2(w), stride, pad, groups)
            if bias is not None:
                y = y + bias[None, :, None, None]
            return y

        def _bn(x, g, b, m, v):
            inv = g * jax.lax.rsqrt(v + BN_EPS)
            return x * inv[None, :, None, None] + (b - m * inv)[None, :, None, None]
        key = jax.random.key(seed)
        ks = jax.random.split(key, 8)
        B, C_in, H, W = (32, 256, 32, 32)
        width, C_out = (64, 256)
        inp = {'x': jax.random.normal(ks[0], (B, C_in, H, W), jnp.float32), 'w1': jax.random.normal(ks[1], (width, C_in, 1, 1), jnp.float32) * 0.05, 'peg_w': jax.random.normal(ks[2], (width, 1, 3, 3), jnp.float32) * 0.1, 'peg_b': jax.random.normal(ks[3], (width,), jnp.float32) * 0.01, 'w2': jax.random.normal(ks[4], (width, width, 3, 3), jnp.float32) * 0.05, 'w3': jax.random.normal(ks[5], (C_out, width, 1, 1), jnp.float32) * 0.05, 'bn1_g': jax.random.uniform(ks[6], (width,), jnp.float32, 0.5, 1.5), 'bn1_b': jnp.zeros((width,), jnp.float32), 'bn1_m': jnp.zeros((width,), jnp.float32), 'bn1_v': jnp.ones((width,), jnp.float32), 'bn2_g': jax.random.uniform(ks[7], (width,), jnp.float32, 0.5, 1.5), 'bn2_b': jnp.zeros((width,), jnp.float32), 'bn2_m': jnp.zeros((width,), jnp.float32), 'bn2_v': jnp.ones((width,), jnp.float32), 'bn3_g': jax.random.uniform(jax.random.fold_in(key, 9), (C_out,), jnp.float32, 0.5, 1.5), 'bn3_b': jnp.zeros((C_out,), jnp.float32), 'bn3_m': jnp.zeros((C_out,), jnp.float32), 'bn3_v': jnp.ones((C_out,), jnp.float32)}
        return inp
    _L1_conv_all = _L1_conv_setup()
    _L1_conv_in = {k: v for k, v in _L1_conv_all.items() if k in ('w1', 'peg_w', 'peg_b', 'w2', 'w3', 'bn1_g', 'bn1_b', 'bn1_m', 'bn1_v', 'bn2_g', 'bn2_b', 'bn2_m', 'bn2_v', 'bn3_g', 'bn3_b', 'bn3_m', 'bn3_v')}
    del _L1_conv_all
    return {'x': x, 'L0_conv_w1': _L0_conv_in['w1'], 'L0_conv_gn1_scale': _L0_conv_in['gn1_scale'], 'L0_conv_gn1_bias': _L0_conv_in['gn1_bias'], 'L0_conv_w_off': _L0_conv_in['w_off'], 'L0_conv_b_off': _L0_conv_in['b_off'], 'L0_conv_w2': _L0_conv_in['w2'], 'L0_conv_gn2_scale': _L0_conv_in['gn2_scale'], 'L0_conv_gn2_bias': _L0_conv_in['gn2_bias'], 'L0_conv_w3': _L0_conv_in['w3'], 'L0_conv_gn3_scale': _L0_conv_in['gn3_scale'], 'L0_conv_gn3_bias': _L0_conv_in['gn3_bias'], 'L1_conv_w1': _L1_conv_in['w1'], 'L1_conv_peg_w': _L1_conv_in['peg_w'], 'L1_conv_peg_b': _L1_conv_in['peg_b'], 'L1_conv_w2': _L1_conv_in['w2'], 'L1_conv_w3': _L1_conv_in['w3'], 'L1_conv_bn1_g': _L1_conv_in['bn1_g'], 'L1_conv_bn1_b': _L1_conv_in['bn1_b'], 'L1_conv_bn1_m': _L1_conv_in['bn1_m'], 'L1_conv_bn1_v': _L1_conv_in['bn1_v'], 'L1_conv_bn2_g': _L1_conv_in['bn2_g'], 'L1_conv_bn2_b': _L1_conv_in['bn2_b'], 'L1_conv_bn2_m': _L1_conv_in['bn2_m'], 'L1_conv_bn2_v': _L1_conv_in['bn2_v'], 'L1_conv_bn3_g': _L1_conv_in['bn3_g'], 'L1_conv_bn3_b': _L1_conv_in['bn3_b'], 'L1_conv_bn3_m': _L1_conv_in['bn3_m'], 'L1_conv_bn3_v': _L1_conv_in['bn3_v']}

def reference(x, L0_conv_w1, L0_conv_gn1_scale, L0_conv_gn1_bias, L0_conv_w_off, L0_conv_b_off, L0_conv_w2, L0_conv_gn2_scale, L0_conv_gn2_bias, L0_conv_w3, L0_conv_gn3_scale, L0_conv_gn3_bias, L1_conv_w1, L1_conv_peg_w, L1_conv_peg_b, L1_conv_w2, L1_conv_w3, L1_conv_bn1_g, L1_conv_bn1_b, L1_conv_bn1_m, L1_conv_bn1_v, L1_conv_bn2_g, L1_conv_bn2_b, L1_conv_bn2_m, L1_conv_bn2_v, L1_conv_bn3_g, L1_conv_bn3_b, L1_conv_bn3_m, L1_conv_bn3_v):
    import jax
    import jax.numpy as jnp

    def _L0_conv_ref(x, w1, gn1_scale, gn1_bias, w_off, b_off, w2, gn2_scale, gn2_bias, w3, gn3_scale, gn3_bias, stride):
        import jax, jax.numpy as jnp
        import numpy as np

        def conv(x, w, stride=1, pad=0):
            return jax.lax.conv_general_dilated(x, w, (stride, stride), [(pad, pad), (pad, pad)], dimension_numbers=('NCHW', 'OIHW', 'NCHW'))

        def group_norm(x, scale, bias, groups=32, eps=1e-05):
            B, C, H, W = x.shape
            xg = x.reshape(B, groups, C // groups, H, W)
            m = xg.mean(axis=(2, 3, 4), keepdims=True)
            v = xg.var(axis=(2, 3, 4), keepdims=True)
            xn = ((xg - m) * jax.lax.rsqrt(v + eps)).reshape(B, C, H, W)
            return xn * scale[None, :, None, None] + bias[None, :, None, None]

        def bilinear_sample(x, py, px):
            B, C, H, W = x.shape
            y0 = jnp.floor(py)
            x0 = jnp.floor(px)
            wy1 = py - y0
            wx1 = px - x0
            xf = x.reshape(B, C, H * W)
            Ksp = py.shape[1:]

            def corner(yi, xi, wy, wx):
                valid = (yi >= 0) & (yi < H) & (xi >= 0) & (xi < W)
                yc = jnp.clip(yi, 0, H - 1).astype(jnp.int32)
                xc = jnp.clip(xi, 0, W - 1).astype(jnp.int32)
                idx = (yc * W + xc).reshape(B, 1, -1)
                v = jnp.take_along_axis(xf, idx, axis=2).reshape(B, C, *Ksp)
                w = (wy * wx * valid).astype(x.dtype)[:, None]
                return v * w
            return corner(y0, x0, 1.0 - wy1, 1.0 - wx1) + corner(y0, x0 + 1, 1.0 - wy1, wx1) + corner(y0 + 1, x0, wy1, 1.0 - wx1) + corner(y0 + 1, x0 + 1, wy1, wx1)
        out = conv(x, w1)
        out = jax.nn.relu(group_norm(out, gn1_scale, gn1_bias))
        om = conv(out, w_off, pad=1) + b_off[None, :, None, None]
        K = 9
        off_x = om[:, :K]
        off_y = om[:, K:2 * K]
        mask = jax.nn.sigmoid(om[:, 2 * K:])
        B, C, H, W = out.shape
        ky, kx = jnp.meshgrid(jnp.arange(3), jnp.arange(3), indexing='ij')
        ky = (ky.reshape(K) - 1).astype(om.dtype)
        kx = (kx.reshape(K) - 1).astype(om.dtype)
        grid_y = jnp.arange(H, dtype=om.dtype)[None, :, None] + ky[:, None, None]
        grid_x = jnp.arange(W, dtype=om.dtype)[None, None, :] + kx[:, None, None]
        py = grid_y[None] + off_y
        px = grid_x[None] + off_x
        sampled = bilinear_sample(out, py, px) * mask[:, None]
        out = jnp.einsum('bckhw,ock->bohw', sampled, w2.reshape(w2.shape[0], w2.shape[1], K))
        out = jax.nn.relu(group_norm(out, gn2_scale, gn2_bias))
        out = conv(out, w3)
        out = group_norm(out, gn3_scale, gn3_bias)
        return jax.nn.relu(out + x)

    def _L1_conv_ref(x, w1, peg_w, peg_b, w2, w3, bn1_g, bn1_b, bn1_m, bn1_v, bn2_g, bn2_b, bn2_m, bn2_v, bn3_g, bn3_b, bn3_m, bn3_v):
        import jax, jax.numpy as jnp
        import numpy as np
        WEIGHT_BITS = 5
        QUANT_BITS = 16
        BN_EPS = 1e-05

        def _quant_weight_pow2(w):
            shift_min = -(2 ** (WEIGHT_BITS - 1) - 2)
            sign = jnp.sign(w)
            p = jnp.clip(jnp.round(jnp.log2(jnp.abs(w) + 1e-20)), shift_min, 0.0)
            wq = sign * jnp.exp2(p)
            return w + jax.lax.stop_gradient(wq - w)

        def _quant_act(x):
            qmax = 2.0 ** (QUANT_BITS - 1) - 1.0
            scale = jnp.maximum(jnp.max(jnp.abs(x)), 1e-12) / qmax
            xq = jnp.round(x / scale) * scale
            return x + jax.lax.stop_gradient(xq - x)

        def _conv(x, w, stride=1, pad=0, groups=1):
            return jax.lax.conv_general_dilated(x, w, (stride, stride), [(pad, pad), (pad, pad)], dimension_numbers=('NCHW', 'OIHW', 'NCHW'), feature_group_count=groups)

        def _shift_conv(x, w, stride=1, pad=0, groups=1, bias=None):
            y = _conv(_quant_act(x), _quant_weight_pow2(w), stride, pad, groups)
            if bias is not None:
                y = y + bias[None, :, None, None]
            return y

        def _bn(x, g, b, m, v):
            inv = g * jax.lax.rsqrt(v + BN_EPS)
            return x * inv[None, :, None, None] + (b - m * inv)[None, :, None, None]
        residual = x
        h = _shift_conv(x, w1)
        h = _shift_conv(h, peg_w, stride=1, pad=1, groups=64, bias=peg_b)
        h = jax.nn.relu(_bn(h, bn1_g, bn1_b, bn1_m, bn1_v))
        h = _shift_conv(h, w2, stride=1, pad=1)
        h = jax.nn.relu(_bn(h, bn2_g, bn2_b, bn2_m, bn2_v))
        h = _shift_conv(h, w3)
        h = _bn(h, bn3_g, bn3_b, bn3_m, bn3_v)
        return jax.nn.relu(h + residual)

    def _gn(v, G=32, eps=1e-05):
        B_, C_, H_, W_ = v.shape
        g = v.reshape(B_, G, C_ // G, H_, W_)
        m = jnp.mean(g, axis=(2, 3, 4), keepdims=True)
        s = jnp.var(g, axis=(2, 3, 4), keepdims=True)
        return ((g - m) / jnp.sqrt(s + eps)).reshape(v.shape)

    def _ln_c(v, eps=1e-06):
        m = jnp.mean(v, axis=1, keepdims=True)
        s = jnp.var(v, axis=1, keepdims=True)
        return (v - m) / jnp.sqrt(s + eps)

    def _ln_t(v, eps=1e-05):
        m = jnp.mean(v, axis=-1, keepdims=True)
        s = jnp.var(v, axis=-1, keepdims=True)
        return (v - m) / jnp.sqrt(s + eps)

    def _to_tokens(v):
        B_, C_, H_, W_ = v.shape
        return v.reshape(B_, C_, H_ * W_).transpose(0, 2, 1)

    def _from_tokens(t, like):
        B_, C_, H_, W_ = like.shape
        return t.transpose(0, 2, 1).reshape(B_, C_, H_, W_)
    x = _L0_conv_ref(x, L0_conv_w1, L0_conv_gn1_scale, L0_conv_gn1_bias, L0_conv_w_off, L0_conv_b_off, L0_conv_w2, L0_conv_gn2_scale, L0_conv_gn2_bias, L0_conv_w3, L0_conv_gn3_scale, L0_conv_gn3_bias, 4)
    x = _L1_conv_ref(x, L1_conv_w1, L1_conv_peg_w, L1_conv_peg_b, L1_conv_w2, L1_conv_w3, L1_conv_bn1_g, L1_conv_bn1_b, L1_conv_bn1_m, L1_conv_bn1_v, L1_conv_bn2_g, L1_conv_bn2_b, L1_conv_bn2_m, L1_conv_bn2_v, L1_conv_bn3_g, L1_conv_bn3_b, L1_conv_bn3_m, L1_conv_bn3_v)
    return x

_drawn_inputs = setup_inputs


def setup_inputs(seed=0):
    import zlib

    import numpy as np

    out = dict(_drawn_inputs(seed))
    spreads = {'L0_conv_gn1_scale': (1.0, 0.2),
     'L0_conv_gn1_bias': (0.0, 0.1),
     'L0_conv_b_off': (0.0, 0.1),
     'L0_conv_gn2_scale': (1.0, 0.2),
     'L0_conv_gn2_bias': (0.0, 0.1),
     'L0_conv_gn3_scale': (1.0, 0.2),
     'L0_conv_gn3_bias': (0.0, 0.1),
     'L1_conv_bn1_b': (0.0, 0.485),
     'L1_conv_bn1_m': (0.0, 0.338),
     'L1_conv_bn1_v': (1.0, 0.6),
     'L1_conv_bn2_b': (0.0, 0.341),
     'L1_conv_bn2_m': (0.0, 0.325),
     'L1_conv_bn2_v': (1.0, 0.6),
     'L1_conv_bn3_b': (0.0, 0.1),
     'L1_conv_bn3_m': (0.0, 0.1),
     'L1_conv_bn3_v': (1.0, 0.6)}
    factors = {'L1_conv_peg_b': 8.0, 'L1_conv_bn1_g': 3.069, 'L1_conv_bn2_g': 2.699}
    for name, (base, spread) in spreads.items():
        noise = np.random.default_rng([zlib.crc32(name.encode()), seed]).standard_normal(out[name].shape)
        drawn = base * np.exp(spread * noise) if base else spread * noise
        out[name] = jnp.asarray(drawn.astype(out[name].dtype))
    for name, factor in factors.items():
        out[name] = (out[name] * factor).astype(out[name].dtype)
    return out
```

```python
from contextlib import ExitStack

import concourse.bass as bass
from concourse import mybir

P = 128
B, C, H, W = 4, 256, 16, 16
HALVES = 2
B2 = B // HALVES
N = H * W
CB = 64
TAPS = 9
OFF = 3 * TAPS
OFF_ROWS = 32
CH = C // P
PIX = B2 * N
T = PIX // P
NQ = N // P
ROWS_Q = H // NQ
GT = TAPS * N
PER_SLOT = 3
HP, WP = H + 2, W + 2
EPS = 1e-5
QMAX = float(2 ** 15 - 1)
ROUND = 1.5 * 2.0 ** 23
SQRT2 = 1.4142135623730951
LEAST_POWER = 2.0 ** -14

F32 = mybir.dt.float32
BF16 = mybir.dt.bfloat16
I32 = mybir.dt.int32
ALU = mybir.AluOpType
ACT = mybir.ActivationFunctionType
AX_X = mybir.AxisListType.X

(V_GN1S, V_GN1B, V_GN2S, V_GN2B, V_GN3S, V_GN3B, V_PEGB, V_BOFF, V_BNG, V_BNB, V_BNM, V_BNV) = (
    0, 1, 2, 3, 4, 6, 8, 9, 10, 14, 18, 22)
V_COLS = 26
Q_W1, Q_PEG, Q_W2, Q_W3 = 0, CH * CB, CH * CB + TAPS, CH * CB + TAPS + TAPS * CB
Q_COLS = Q_W3 + C
C_ID, C_AVG2, C_DEV2, C_AVG8, C_DEV8, C_COORD = 0, P, 2 * P, 3 * P, 4 * P, 5 * P
C_COLS = 5 * P + H


def build(nc, x, first, consts, woff, grid, w2, w3, wq, out):
    with ExitStack() as ctx:
        def sb(name, shape, dt=F32):
            return ctx.enter_context(nc.sbuf_tensor(name, shape, dt))

        def ps(name, shape):
            return ctx.enter_context(nc.psum_tensor(name, shape, F32))

        def sem(name):
            return ctx.enter_context(nc.semaphore(name))

        x_sb = sb("x_sb", [P, CH, B, N])
        first_sb = sb("first_sb", [P, CH * CB + V_COLS])
        w1_sb = first_sb[:, 0:CH * CB].rearrange("p (c o) -> p c o", c=CH)
        vec = first_sb[:, CH * CB:CH * CB + V_COLS]
        consts_sb = sb("consts_sb", [P, C_COLS])
        ident = consts_sb[:, C_ID:C_ID + P]
        avg2 = consts_sb[:, C_AVG2:C_AVG2 + P]
        dev2 = consts_sb[:, C_DEV2:C_DEV2 + P]
        avg8 = consts_sb[:, C_AVG8:C_AVG8 + P]
        dev8 = consts_sb[:, C_DEV8:C_DEV8 + P]
        coord = consts_sb[:, C_COORD:C_COORD + H]
        woff_sb = sb("woff_sb", [P, TAPS, CB])
        grid_sb = sb("grid_sb", [CB, PIX])
        w2_sb = sb("w2_sb", [P, TAPS * CB])
        w3_sb = sb("w3_sb", [P, C])
        wq_sb = sb("wq_sb", [P, Q_COLS])
        wq_mag = sb("wq_mag", [P, Q_COLS])
        wq_sign = sb("wq_sign", [P, Q_COLS])
        wqb = sb("wqb", [P, Q_COLS], BF16)
        w2q = sb("w2q", [P, TAPS, HALVES, CB], BF16)
        pegq = sb("pegq", [P, TAPS, P], BF16)

        feat = sb("feat", [P, B2, HP, WP])
        feat_flat = sb("feat_flat", [P, PIX])
        om_sb = sb("om_sb", [CB, PIX])
        omt_sb = sb("omt_sb", [P, T, HALVES, OFF_ROWS])
        mask = sb("mask", [P, T, HALVES, TAPS])
        hats = sb("hats", [P, T, HALVES, 2, TAPS, H])
        g_rows = [sb(f"g_rows{i}", [P, TAPS, H, W]) for i in range(3)]
        g_cols = [sb(f"g_cols{i}", [P, TAPS * NQ, P]) for i in range(4)]
        v_sb = sb("v_sb", [P, B, NQ, TAPS, CB])
        feat2 = sb("feat2", [P, PIX])
        y0 = sb("y0", [P, CH, B, N])
        act = sb("act", [P, PIX])
        quot = sb("quot", [P, CH * B * N])
        n1_hi = sb("n1_hi", [P, CH, B, N], BF16)
        n1_lo = sb("n1_lo", [P, CH, B, N], BF16)
        pads = [sb(f"pad{i}", [P, B2, HP, WP], BF16) for i in range(4)]
        n4_hi = sb("n4_hi", [P, PIX], BF16)
        n4_lo = sb("n4_lo", [P, PIX], BF16)
        res = sb("res", [P, CH, B * N])
        warm = sb("warm", [P, 512], BF16)

        stats = sb("stats", [P, 8, 6])
        mv = sb("mv", [P, 8, 2])
        dev_sb = sb("dev_sb", [P, 8])
        var = sb("var", [P, 8])
        std = sb("std", [P, 8])
        rstd = sb("rstd", [P, 8])
        gn_scale = sb("gn_scale", [P, 8])
        gn_bias = sb("gn_bias", [P, 8])
        bn_std = sb("bn_std", [P, 4])
        bn_inv = sb("bn_inv", [P, 4])
        bn_off = sb("bn_off", [P, 4])
        mx = sb("mx", [P, 8])
        scl = sb("scl", [P, 24])
        eps_sb = sb("eps_sb", [P, 1])

        slot = [ps(f"slot{i}", [P, 1024]) for i in range(3)]
        acc = ps("acc", [P, PIX])
        misc = ps("misc", [P, 512])

        first_in, consts_in, woff_in, grid_in, w2_in, w3_in, wq_in, stored = (
            sem(n) for n in ("first_in", "consts_in", "woff_in", "grid_in", "w2_in", "w3_in", "wq_in",
                             "stored"))
        x_in = [[sem(f"x_in{h}{c}") for c in range(CH)] for h in range(HALVES)]
        pads_zero = sem("pads_zero")
        conv1_done = sem("conv1_done")
        mv_ready = sem("mv_ready")
        avg_done = sem("avg_done")
        sq_ready = sem("sq_ready")
        var_ready = sem("var_ready")
        std_ready = sem("std_ready")
        gn_ready = sem("gn_ready")
        feat_ready = sem("feat_ready")
        flat_ready = sem("flat_ready")
        om_done = sem("om_done")
        om_ready = sem("om_ready")
        omt_done = sem("omt_done")
        omt_ready = sem("omt_ready")
        mask_ready = sem("mask_ready")
        diff_ready = sem("diff_ready")
        abs_ready = sem("abs_ready")
        v_done = sem("v_done")
        v_ready = sem("v_ready")
        hats_ready = sem("hats_ready")
        g_ready = sem("g_ready")
        turned = sem("turned")
        g_copied = sem("g_copied")
        sampled = sem("sampled")
        feat2_ready = sem("feat2_ready")
        conv3_done = sem("conv3_done")
        norm3_ready = sem("norm3_ready")
        sign_ready = sem("sign_ready")
        wq_ready = sem("wq_ready")
        placed = sem("placed")
        max_ready = sem("max_ready")
        max_spread = sem("max_spread")
        scale_ready = sem("scale_ready")
        quot_ready = sem("quot_ready")
        parts_ready = sem("parts_ready")
        qconv_done = sem("qconv_done")
        act_ready = sem("act_ready")
        sum_ready = sem("sum_ready")
        res_ready = sem("res_ready")
        chain = sem("dve_chain")
        pool_chain = sem("pool_chain")
        act_chain = sem("act_chain")

        block = ctx.enter_context(nc.Block())

        def taps(tile, k):
            dy, dx = k // 3, k % 3
            return tile[:, :, dy:dy + H, dx:dx + W]

        x_v = x.rearrange("(h b) (c p) n -> c h p b n", h=HALVES, c=CH)
        out_v = out.rearrange("b (c p) n -> c p b n", c=CH)

        @block.sync
        def _(sp):
            sp.dma_start(first_sb[:], first).then_inc(first_in, 16)
            for h in range(HALVES):
                for c in range(CH):
                    sp.dma_start(x_sb[:, c, B2 * h:B2 * h + B2, :], x_v[c, h]).then_inc(x_in[h][c], 16)
            sp.dma_start(consts_sb[:], consts).then_inc(consts_in, 16)
            sp.dma_start(woff_sb[:], woff).then_inc(woff_in, 16)
            sp.dma_start(grid_sb[:], grid).then_inc(grid_in, 16)
            sp.dma_start(wq_sb[:], wq).then_inc(wq_in, 16)
            sp.dma_start(w2_sb[:], w2).then_inc(w2_in, 16)
            sp.dma_start(w3_sb[:], w3).then_inc(w3_in, 16)
            for c in range(CH):
                sp.wait_ge(res_ready, c + 1)
                sp.dma_start(out_v[c], res[:, c, :].rearrange("p (b n) -> p b n", b=B)).then_inc(stored, 16)
            sp.wait_ge(stored, 16 * CH)

        @block.gpsimd
        def _(pool):
            nc.gpsimd.memset(feat[:], 0.0).then_inc(pads_zero, 1)
            for t in pads:
                nc.gpsimd.memset(t[:], 0.0).then_inc(pads_zero, 1)
            nc.gpsimd.memset(w2q[:], 0.0).then_inc(pads_zero, 1)
            pool.wait_ge(feat_ready, 2)
            nc.gpsimd.tensor_copy(feat_flat[:].rearrange("p (b y x) -> p b y x", b=B2, y=H),
                                  feat[:, :, 1:1 + H, 1:1 + W]).then_inc(flat_ready, 1)
            pool.wait_ge(consts_in, 16)
            pool.wait_ge(wq_ready, 1)
            nc.gpsimd.tensor_tensor(
                pegq[:], ident.unsqueeze(1).to_broadcast([P, TAPS, P]),
                wqb[:, Q_PEG:Q_PEG + TAPS].unsqueeze(2).to_broadcast([P, TAPS, P]), ALU.mult).then_inc(placed, 1)
            pool.wait_ge(pads_zero, 6)
            for h in range(HALVES):
                rows = slice(CB * h, CB * h + CB)
                pool.wait_ge(placed, h + 1)
                nc.gpsimd.tensor_copy(w2q[rows, :, h, :],
                                      wqb[rows, Q_W2:Q_W2 + TAPS * CB].rearrange("p (k o) -> p k o", k=TAPS)
                                      ).then_inc(placed, 1)
            pool.wait_ge(placed, 1 + HALVES)
            for t in range(T):
                pool.wait_ge(abs_ready, 2 * t + 2)
                pool.wait_ge(mask_ready, 1)
                nc.gpsimd.tensor_tensor(hats[:, t, :, 1], hats[:, t, :, 1],
                                        mask[:, t].unsqueeze(3).to_broadcast([P, HALVES, TAPS, H]),
                                        ALU.mult).then_inc(hats_ready, 1)

        @block.tensor
        def _(pe):
            pe.wait_ge(first_in, 16)
            for h in range(HALVES):
                for c in range(CH):
                    pe.wait_ge(x_in[h][c], 16)
                    mm = nc.tensor.matmul(acc[CB * h:CB * h + CB, :], w1_sb[:, c, :],
                                          x_sb[:, c, B2 * h:B2 * h + B2, :], start=(c == 0), stop=(c == CH - 1))
            mm.then_inc(conv1_done, 1)

            def group_sums(done, n, avg, dev):
                pe.wait_ge(mv_ready, done)
                if done == 1:
                    pe.wait_ge(consts_in, 16)
                nc.tensor.matmul(misc[:, 0:n], avg, mv[:, 0:n, 0], start=True, stop=True)
                nc.tensor.matmul(misc[:, 16:16 + n], dev, mv[:, 0:n, 0], start=True, stop=True).then_inc(avg_done, 1)
                pe.wait_ge(sq_ready, done)
                nc.tensor.matmul(misc[:, 32:32 + n], avg, var[:, 0:n], start=True, stop=True).then_inc(avg_done, 1)

            group_sums(1, B2, avg2, dev2)

            pe.wait_ge(woff_in, 16)
            pe.wait_ge(feat_ready, 2)
            for k in range(TAPS):
                mm = nc.tensor.matmul(slot[0][0:CB, 0:PIX], woff_sb[:, k, :], taps(feat, k),
                                      start=(k == 0), stop=(k == TAPS - 1))
            mm.then_inc(om_done, 1)
            pe.wait_ge(w2_in, 16)
            pe.wait_ge(flat_ready, 1)

            def make_v(i):
                b, q = i // NQ, i % NQ
                h, b2 = b // B2, b % B2
                rows = slice(CB * h, CB * h + CB)
                if i >= 2:
                    pe.wait_ge(v_ready, i - 1)
                at = N * b2 + P * q
                lhs = feat_flat[rows, at:at + P]
                nc.tensor.matmul(slot[1 + i % 2][:, 0:512], lhs, w2_sb[rows, 0:512], start=True, stop=True)
                nc.tensor.matmul(slot[1 + i % 2][:, 512:TAPS * CB], lhs, w2_sb[rows, 512:TAPS * CB],
                                 start=True, stop=True).then_inc(v_done, 1)

            make_v(0)
            pe.wait_ge(om_ready, 1)
            for t in range(T):
                mm = nc.tensor.transpose(misc[:, CB * t:CB * t + CB], om_sb[:, P * t:P * t + P], ident[0:CB, 0:CB])
            mm.then_inc(omt_done, 1)
            for i in range(1, B * NQ):
                make_v(i)

            def turn(i):
                pe.wait_ge(g_ready, i + 1)
                for j in range(TAPS // PER_SLOT):
                    if i == 0 and j == 1:
                        pe.wait_ge(v_ready, B * NQ)
                    if i > 0:
                        pe.wait_ge(g_copied, 3 * (i - 1) + j + 1)
                    for k in range(PER_SLOT * j, PER_SLOT * j + PER_SLOT):
                        for q in range(NQ):
                            at = P * (NQ * (k - PER_SLOT * j) + q)
                            mm = nc.tensor.transpose(slot[j][:, at:at + P],
                                                     g_rows[i % 3][:, k, ROWS_Q * q:ROWS_Q * q + ROWS_Q, :], ident)
                    mm.then_inc(turned, 1)

            def sample(t):
                for j in range(TAPS // PER_SLOT):
                    pe.wait_ge(g_copied, 3 * (2 * t + 1) + j + 1)
                    for k in range(PER_SLOT * j, PER_SLOT * j + PER_SLOT):
                        for q in range(NQ):
                            for h in range(HALVES):
                                b = B2 * h + t // NQ
                                first_k, last_k = k == 0 and q == 0, k == TAPS - 1 and q == NQ - 1
                                mm = nc.tensor.matmul(
                                    acc[CB * h:CB * h + CB, P * t:P * t + P], v_sb[:, b, q, k, :],
                                    g_cols[(2 * t + h) % 4][:, NQ * k + q, :], start=first_k, stop=last_k)
                mm.then_inc(sampled, 1)

            for i in range(2 * T):
                turn(i)
                if i % 2 == 0 and i > 0:
                    sample(i // 2 - 1)
            sample(T - 1)

            group_sums(2, B2, avg2, dev2)

            pe.wait_ge(w3_in, 16)
            pe.wait_ge(feat2_ready, 2)
            for c in range(CH):
                for h in range(HALVES):
                    rows = slice(CB * h, CB * h + CB)
                    mm = nc.tensor.matmul(slot[c][:, PIX * h:PIX * h + PIX], w3_sb[rows, P * c:P * c + P],
                                          feat2[rows, :], start=True, stop=True)
                mm.then_inc(conv3_done, 1)
            group_sums(3, CH * B, avg8, dev8)

            def spread_max(n):
                pe.wait_ge(max_ready, n)
                nc.tensor.transpose(misc[:, 0:P], mx[:, n - 1:n].to_broadcast([P, P]), ident).then_inc(max_spread, 1)

            spread_max(1)
            pe.wait_ge(placed, 3)
            for p in range(2):
                for c in range(CH):
                    pe.wait_ge(parts_ready, CH * p + c + 1)
                    for h in range(HALVES):
                        part = (n1_hi, n1_lo)[p]
                        mm = nc.tensor.matmul(acc[CB * h:CB * h + CB, :],
                                              wqb[:, Q_W1 + CB * c:Q_W1 + CB * c + CB],
                                              part[:, c, B2 * h:B2 * h + B2, :],
                                              start=(p == 0 and c == 0), stop=(p == 1 and c == CH - 1))
            mm.then_inc(qconv_done, 1)
            spread_max(2)

            def window_conv(dst, weights, hi, lo, ready):
                for p, part in enumerate((hi, lo)):
                    pe.wait_ge(parts_ready, ready + p)
                    for k in range(TAPS):
                        mm = nc.tensor.matmul(dst, weights(k), taps(part, k), start=(p == 0 and k == 0),
                                              stop=(p == 1 and k == TAPS - 1))
                mm.then_inc(qconv_done, 1)

            window_conv(slot[2][:, 0:PIX], lambda k: pegq[:, k, :], pads[0], pads[1], 2 * CH + 1)
            spread_max(3)
            window_conv(acc[:], lambda k: w2q[:, k].rearrange("p h o -> p (h o)"), pads[2], pads[3], 2 * CH + 3)
            spread_max(4)
            for c in range(CH):
                for p, part in enumerate((n4_hi, n4_lo)):
                    pe.wait_ge(parts_ready, 2 * CH + 5 + p)
                    for h in range(HALVES):
                        rows = slice(CB * h, CB * h + CB)
                        mm = nc.tensor.matmul(slot[c][:, PIX * h:PIX * h + PIX],
                                              wqb[rows, Q_W3 + P * c:Q_W3 + P * c + P], part[rows, :],
                                              start=(p == 0), stop=(p == 1))
                mm.then_inc(qconv_done, 1)

        @block.scalar
        def _(a):
            def root(n, cols):
                a.wait_ge(var_ready, cols[0])
                nc.scalar.activation(std[:, 0:n], var[:, 0:n], ACT.Sqrt).then_inc(std_ready, 1)

            a.wait_ge(var_ready, 1)
            nc.scalar.activation(bn_std[:], bn_std[:], ACT.Sqrt).then_inc(std_ready, 1)
            root(B2, (2,))
            a.wait_ge(gn_ready, 1)
            a.wait_ge(pads_zero, 1)
            for b2 in range(B2):
                nc.scalar.activation(feat[:, b2, 1:1 + H, 1:1 + W],
                                     acc[:, N * b2:N * b2 + N].rearrange("p (y x) -> p y x", y=H), ACT.Relu,
                                     bias=gn_bias[:, b2:b2 + 1], scale=gn_scale[:, b2:b2 + 1]).then_inc(feat_ready, 1)
            a.wait_ge(wq_in, 16)
            nc.scalar.activation(wq_sign[:], wq_sb[:], ACT.Sign).then_inc(sign_ready, 1)
            a.wait_ge(omt_done, 1)
            nc.scalar.activation(omt_sb[:].rearrange("p t h o -> p (t h o)"), misc[:, 0:T * CB],
                                 ACT.Copy).then_inc(omt_ready, 1)
            a.wait_ge(omt_ready, 1)
            nc.scalar.activation(mask[:], omt_sb[:, :, :, 2 * TAPS:OFF], ACT.Sigmoid).then_inc(mask_ready, 1)

            def copy_v(i):
                a.wait_ge(v_done, i + 1)
                nc.scalar.activation(v_sb[:, i // NQ, i % NQ].rearrange("p k o -> p (k o)"),
                                     slot[1 + i % 2][:, 0:TAPS * CB], ACT.Copy).then_inc(v_ready, 1)

            def hat(t):
                a.wait_ge(diff_ready, t + 1)
                v = hats[:, t].rearrange("p h a k y -> p (h a k y)")
                nc.scalar.activation(v, v, ACT.Abs).then_inc(abs_ready, 1)
                a.wait_ge(abs_ready, 2 * t + 1)
                nc.scalar.activation(v, v, ACT.Relu, bias=1.0, scale=-1.0).then_inc(abs_ready, 1)

            for t in range(T):
                hat(t)
                copy_v(2 * t)
                copy_v(2 * t + 1)
            for i in range(2 * T):
                for j in range(TAPS // PER_SLOT):
                    a.wait_ge(turned, 3 * i + j + 1)
                    if i >= 4:
                        a.wait_ge(sampled, i // 2 - 1)
                    width = PER_SLOT * NQ * P
                    nc.scalar.activation(g_cols[i % 4][:, PER_SLOT * NQ * j:PER_SLOT * NQ * (j + 1), :]
                                         .rearrange("p k n -> p (k n)"), slot[j][:, 0:width],
                                         ACT.Copy).then_inc(g_copied, 1)
            root(B2, (3,))
            a.wait_ge(gn_ready, 2)
            for b2 in range(B2):
                nc.scalar.activation(feat2[:, N * b2:N * b2 + N], acc[:, N * b2:N * b2 + N], ACT.Relu,
                                     bias=gn_bias[:, b2:b2 + 1], scale=gn_scale[:, b2:b2 + 1]).then_inc(feat2_ready, 1)
            root(CH * B, (4,))
            a.wait_ge(gn_ready, 3)
            for i in range(CH * B):
                c, b = i // B, i % B
                nc.scalar.activation(y0[:, c, b, :], slot[c][:, N * b:N * b + N], ACT.Identity,
                                     bias=gn_bias[:, i:i + 1], scale=gn_scale[:, i:i + 1]).then_inc(norm3_ready, 1)

            def divide(n, dst, src, relu=False):
                a.wait_ge(scale_ready, n)
                nc.scalar.activation(dst, src, ACT.Identity, scale=scl[:, 4 * n:4 * n + 1],
                                     bias=scl[:, 0:1]).then_inc(quot_ready, 1)

            for c in range(CH):
                divide(1, quot[:, B * N * c:B * N * c + B * N], y0[:, c].rearrange("p b n -> p (b n)"))
            a.wait_ge(parts_ready, 2 * CH)
            divide(2, quot[:, 0:PIX], acc[:])
            for n, src in ((0, slot[2][:, 0:PIX]), (1, acc[:])):
                a.wait_ge(qconv_done, 2 + n)
                a.wait_ge(sum_ready, n + 1)
                nc.scalar.activation(act[:], src, ACT.Relu, bias=bn_off[:, n:n + 1],
                                     scale=scl[:, 4 * (2 + n) + 2:4 * (2 + n) + 3]).then_inc(act_ready, 1)
                a.wait_ge(act_ready, n + 1)
                a.wait_ge(parts_ready, 2 * CH + 2 + 2 * n)
                divide(3 + n, quot[:, 0:PIX], act[:])
            for c in range(CH):
                a.wait_ge(norm3_ready, CH * B + c + 1)
                nc.scalar.activation(res[:, c, :], res[:, c, :], ACT.Relu, bias=bn_off[:, 2 + c:3 + c]
                                     ).then_inc(res_ready, 1)

        @block.vector
        def _(dve):
            count = [0]

            def settle(ins):
                count[0] += 1
                ins.then_inc(chain, 1)
                dve.wait_ge(chain, count[0])

            tt, ts, stt = nc.vector.tensor_tensor, nc.vector.tensor_scalar, nc.vector.scalar_tensor_tensor
            dve.wait_ge(first_in, 16)
            ts(bn_std[:], vec[:, V_BNV:V_BNV + 4], EPS, None, ALU.add).then_inc(var_ready, 1)
            settle(nc.vector.memset(scl[:, 0:1], ROUND))
            dve.wait_ge(std_ready, 1)
            settle(nc.vector.reciprocal(bn_std[:], bn_std[:]))
            settle(tt(bn_inv[:], bn_std[:], vec[:, V_BNG:V_BNG + 4], ALU.mult))
            settle(tt(bn_off[:], bn_inv[:], vec[:, V_BNM:V_BNM + 4], ALU.mult))
            settle(tt(bn_off[:], vec[:, V_BNB:V_BNB + 4], bn_off[:], ALU.subtract))
            settle(stt(bn_off[:, 0:1], bn_inv[:, 0:1], vec[:, V_PEGB:V_PEGB + 1], bn_off[:, 0:1], ALU.mult, ALU.add))

            def moments(n, src):
                for i in range(n):
                    last = nc.vector.bn_stats(stats[:, i, :], src(i))
                settle(last)
                for i in range(n):
                    last = nc.vector.bn_aggr(mv[:, i, :], stats[:, i, :])
                last.then_inc(mv_ready, 1)

            def norm(done, n, gamma, beta):
                dve.wait_ge(avg_done, 2 * done - 1)
                settle(nc.vector.tensor_copy(dev_sb[:, 0:n], misc[:, 16:16 + n]))
                settle(tt(dev_sb[:, 0:n], dev_sb[:, 0:n], dev_sb[:, 0:n], ALU.mult))
                tt(var[:, 0:n], dev_sb[:, 0:n], mv[:, 0:n, 1], ALU.add).then_inc(sq_ready, 1)
                dve.wait_ge(avg_done, 2 * done)
                ts(var[:, 0:n], misc[:, 32:32 + n], EPS, None, ALU.add).then_inc(var_ready, 1)
                dve.wait_ge(std_ready, done + 1)
                settle(nc.vector.reciprocal(rstd[:, 0:n], std[:, 0:n]))
                settle(tt(gn_scale[:, 0:n], rstd[:, 0:n], gamma, ALU.mult))
                settle(tt(dev_sb[:, 0:n], gn_scale[:, 0:n], misc[:, 0:n], ALU.mult))
                tt(gn_bias[:, 0:n], beta, dev_sb[:, 0:n], ALU.subtract).then_inc(gn_ready, 1)

            dve.wait_ge(conv1_done, 1)
            moments(B2, lambda i: acc[:, N * i:N * i + N])
            norm(1, B2, vec[:, V_GN1S:V_GN1S + 1].to_broadcast([P, B2]), vec[:, V_GN1B:V_GN1B + 1].to_broadcast([P, B2]))

            dve.wait_ge(wq_in, 16)
            settle(ts(wq_mag[:].bitcast(I32), wq_sb[:].bitcast(I32), 0x7FFFFFFF, None, ALU.bitwise_and))
            settle(ts(wq_mag[:], wq_mag[:], 1e-20, SQRT2, ALU.add, ALU.mult))
            settle(ts(wq_mag[:].bitcast(I32), wq_mag[:].bitcast(I32), 0x7F800000, None, ALU.bitwise_and))
            settle(ts(wq_mag[:], wq_mag[:], LEAST_POWER, 1.0, ALU.max, ALU.min))
            dve.wait_ge(sign_ready, 1)
            tt(wqb[:], wq_mag[:], wq_sign[:], ALU.mult).then_inc(wq_ready, 1)

            dve.wait_ge(grid_in, 16)
            dve.wait_ge(om_done, 1)
            stt(om_sb[:], slot[0][0:CB, 0:PIX], vec[0:CB, V_BOFF:V_BOFF + 1], grid_sb[:], ALU.add,
                ALU.add).then_inc(om_ready, 1)
            dve.wait_ge(omt_ready, 1)
            for t in range(T):
                tt(hats[:, t].rearrange("p h a k y -> p h (a k) y"),
                   omt_sb[:, t, :, 0:2 * TAPS].unsqueeze(3).to_broadcast([P, HALVES, 2 * TAPS, H]),
                   coord.unsqueeze(1).unsqueeze(1).to_broadcast([P, HALVES, 2 * TAPS, H]),
                   ALU.subtract).then_inc(diff_ready, 1)
            for i in range(2 * T):
                t, h = i // 2, i % 2
                dve.wait_ge(hats_ready, t + 1)
                if i >= 3:
                    dve.wait_ge(turned, 3 * (i - 2))
                tt(g_rows[i % 3][:], hats[:, t, h, 1].unsqueeze(3).to_broadcast([P, TAPS, H, W]),
                   hats[:, t, h, 0].unsqueeze(2).to_broadcast([P, TAPS, H, W]), ALU.mult).then_inc(g_ready, 1)

            dve.wait_ge(sampled, T)
            moments(B2, lambda i: acc[:, N * i:N * i + N])
            norm(2, B2, vec[:, V_GN2S:V_GN2S + 1].to_broadcast([P, B2]), vec[:, V_GN2B:V_GN2B + 1].to_broadcast([P, B2]))

            dve.wait_ge(conv3_done, CH)
            moments(CH * B, lambda i: slot[i // B][:, N * (i % B):N * (i % B) + N])

            def by_half(at):
                return vec[:, at:at + CH].unsqueeze(2).to_broadcast([P, CH, B])

            n = CH * B

            def pair(t):
                return t.rearrange("p (c b) -> p c b", c=CH)

            dve.wait_ge(avg_done, 5)
            settle(nc.vector.tensor_copy(dev_sb[:, 0:n], misc[:, 16:16 + n]))
            settle(tt(dev_sb[:, 0:n], dev_sb[:, 0:n], dev_sb[:, 0:n], ALU.mult))
            tt(var[:, 0:n], dev_sb[:, 0:n], mv[:, 0:n, 1], ALU.add).then_inc(sq_ready, 1)
            dve.wait_ge(avg_done, 6)
            ts(var[:, 0:n], misc[:, 32:32 + n], EPS, None, ALU.add).then_inc(var_ready, 1)
            dve.wait_ge(std_ready, 4)
            settle(nc.vector.reciprocal(rstd[:], std[:]))
            settle(tt(pair(gn_scale[:]), pair(rstd[:]), by_half(V_GN3S), ALU.mult))
            settle(tt(dev_sb[:], gn_scale[:], misc[:, 0:n], ALU.mult))
            tt(pair(gn_bias[:]), by_half(V_GN3B), pair(dev_sb[:]), ALU.subtract).then_inc(gn_ready, 1)

            for i in range(CH * B):
                c, b = i // B, i % B
                dve.wait_ge(norm3_ready, i + 1)
                settle(tt(y0[:, c, b, :], y0[:, c, b, :], x_sb[:, c, b, :], ALU.add))
                last = ts(y0[:, c, b, :], y0[:, c, b, :], 0.0, None, ALU.max)
            settle(last)
            nc.vector.tensor_reduce(mx[:, 0:1], y0[:].rearrange("p c b n -> p (c b n)"), AX_X,
                                    ALU.max).then_inc(max_ready, 1)

            def scale_of(n, unit):
                inv, s = scl[:, 4 * n:4 * n + 1], scl[:, 4 * n + 1:4 * n + 2]
                dve.wait_ge(max_spread, n)
                settle(nc.vector.tensor_reduce(s, misc[:, 0:P], AX_X, ALU.max))
                if unit is not None:
                    settle(tt(s, s, unit, ALU.mult))
                settle(ts(s, s, 1e-12, 1.0 / QMAX, ALU.max, ALU.mult))
                last = nc.vector.reciprocal(inv, s)
                if unit is not None:
                    settle(last)
                    last = tt(inv, inv, unit, ALU.mult)
                last.then_inc(scale_ready, 1)

            def split(n_quot, src, hi, lo):
                dve.wait_ge(quot_ready, n_quot)
                settle(ts(hi, src, ROUND, None, ALU.subtract))
                hi_done = count[0]
                stt(lo, src, ROUND, hi, ALU.subtract, ALU.subtract).then_inc(parts_ready, 1)
                return hi_done

            scale_of(1, None)
            for c in range(CH):
                dve.wait_ge(quot_ready, c + 1)
                ts(n1_hi[:, c].rearrange("p b n -> p (b n)"), quot[:, B * N * c:B * N * c + B * N], ROUND, None,
                   ALU.subtract).then_inc(parts_ready, 1)
            for c in range(CH):
                dve.wait_ge(parts_ready, c + 1)
                stt(n1_lo[:, c].rearrange("p b n -> p (b n)"), quot[:, B * N * c:B * N * c + B * N], ROUND,
                    n1_hi[:, c].rearrange("p b n -> p (b n)"), ALU.subtract, ALU.subtract).then_inc(parts_ready, 1)

            def unpadded(t):
                return t[:, :, 1:1 + H, 1:1 + W]

            def as_image(t):
                return t.rearrange("p (b y x) -> p b y x", b=B2, y=H)

            def parts(n, hi, lo):
                img = as_image(quot[:, 0:PIX])
                dve.wait_ge(quot_ready, CH + n)
                ts(hi, img, ROUND, None, ALU.subtract).then_inc(parts_ready, 1)
                dve.wait_ge(parts_ready, 2 * CH + 2 * n - 1)
                for b2 in range(B2):
                    last = stt(lo[:, b2], img[:, b2], ROUND, hi[:, b2], ALU.subtract, ALU.subtract)
                last.then_inc(parts_ready, 1)

            dve.wait_ge(qconv_done, 1)
            nc.vector.tensor_reduce(mx[:, 1:2], acc[:], AX_X, ALU.max,
                                    apply_absolute_value=True).then_inc(max_ready, 1)
            scale_of(2, scl[:, 5:6])
            tt(scl[:, 10:11], scl[:, 9:10], bn_inv[:, 0:1], ALU.mult).then_inc(sum_ready, 1)
            dve.wait_ge(pads_zero, 5)
            parts(1, unpadded(pads[0]), unpadded(pads[1]))
            dve.wait_ge(act_ready, 1)
            nc.vector.tensor_reduce(mx[:, 2:3], act[:], AX_X, ALU.max).then_inc(max_ready, 1)
            scale_of(3, None)
            tt(scl[:, 14:15], scl[:, 13:14], bn_inv[:, 1:2], ALU.mult).then_inc(sum_ready, 1)
            parts(2, unpadded(pads[2]), unpadded(pads[3]))
            dve.wait_ge(act_ready, 2)
            nc.vector.tensor_reduce(mx[:, 3:4], act[:], AX_X, ALU.max).then_inc(max_ready, 1)
            scale_of(4, None)
            ts(scl[:, 18:20], bn_inv[:, 2:4], scl[:, 17:18], None, ALU.mult).then_inc(sum_ready, 1)
            parts(3, as_image(n4_hi[:]), as_image(n4_lo[:]))
            dve.wait_ge(sum_ready, 3)
            for c in range(CH):
                dve.wait_ge(qconv_done, 4 + c)
                stt(res[:, c, :], slot[c][:], scl[:, 18 + c:19 + c], y0[:, c].rearrange("p b n -> p (b n)"),
                    ALU.mult, ALU.add).then_inc(norm3_ready, 1)


def kernel(**inputs):
    import numpy as np
    import concourse.bacc as bacc
    from concourse.bass_utils import run_bass_kernel_spmd as run

    f = np.float32
    a = {k: np.asarray(v) for k, v in inputs.items()}

    first = np.zeros((P, CH * CB + V_COLS), f)
    first[:, 0:CH * CB] = a["L0_conv_w1"][:, :, 0, 0].reshape(CB, CH, P).transpose(2, 1, 0).reshape(P, CH * CB)
    vec = first[:, CH * CB:]

    def both(col, v):
        vec[:CB, col] = v
        vec[CB:, col] = v

    for col, name in ((V_GN1S, "L0_conv_gn1_scale"), (V_GN1B, "L0_conv_gn1_bias"), (V_GN2S, "L0_conv_gn2_scale"),
                      (V_GN2B, "L0_conv_gn2_bias"), (V_PEGB, "L1_conv_peg_b")):
        both(col, a[name])
    for col, name in ((V_GN3S, "L0_conv_gn3_scale"), (V_GN3B, "L0_conv_gn3_bias")):
        vec[:, col:col + CH] = a[name].reshape(CH, P).T
    for h in range(HALVES):
        vec[OFF_ROWS * h:OFF_ROWS * h + OFF, V_BOFF] = a["L0_conv_b_off"]
    for col, p in ((V_BNG, "g"), (V_BNB, "b"), (V_BNM, "m"), (V_BNV, "v")):
        both(col, a["L1_conv_bn1_" + p])
        both(col + 1, a["L1_conv_bn2_" + p])
        vec[:, col + 2:col + 4] = a["L1_conv_bn3_" + p].reshape(CH, P).T

    consts = np.zeros((P, C_COLS), f)
    eye = np.eye(P, dtype=f)
    consts[:, C_ID:C_ID + P] = eye
    for g, at_avg, at_dev in ((2, C_AVG2, C_DEV2), (8, C_AVG8, C_DEV8)):
        mean = np.kron(np.eye(P // g, dtype=f), np.full((g, g), 1.0 / g, f))
        consts[:, at_avg:at_avg + P] = mean
        consts[:, at_dev:at_dev + P] = eye - mean
    consts[:, C_COORD:C_COORD + H] = np.arange(H, dtype=f)

    woff = np.zeros((HALVES, CB, TAPS, HALVES, OFF_ROWS), f)
    for h in range(HALVES):
        woff[h, :, :, h, 0:OFF] = a["L0_conv_w_off"].reshape(OFF, CB, TAPS).transpose(1, 2, 0)
    grid = np.zeros((HALVES, OFF_ROWS, B2, H, W), f)
    for k in range(TAPS):
        grid[:, k] = np.arange(W, dtype=f) + (k % 3 - 1)
        grid[:, TAPS + k] = (np.arange(H, dtype=f) + (k // 3 - 1))[:, None]
    w2 = np.zeros((HALVES, CB, TAPS * CB), f)
    w2[:] = a["L0_conv_w2"].reshape(CB, CB, TAPS).transpose(1, 2, 0).reshape(CB, TAPS * CB)
    w3 = np.zeros((HALVES, CB, C), f)
    w3[:] = a["L0_conv_w3"][:, :, 0, 0].T
    wq = np.zeros((HALVES, CB, Q_COLS), f)
    wq.reshape(P, Q_COLS)[:, Q_W1:Q_W1 + CH * CB] = a["L1_conv_w1"][:, :, 0, 0].reshape(CB, CH, P).transpose(
        2, 1, 0).reshape(P, CH * CB)
    wq[:, :, Q_PEG:Q_PEG + TAPS] = a["L1_conv_peg_w"].reshape(CB, TAPS)
    wq[:, :, Q_W2:Q_W2 + TAPS * CB] = a["L1_conv_w2"].reshape(CB, CB, TAPS).transpose(1, 2, 0).reshape(CB, TAPS * CB)
    wq[:, :, Q_W3:Q_W3 + C] = a["L1_conv_w3"][:, :, 0, 0].T

    arrays = {
        "x": np.ascontiguousarray(a["x"]).reshape(B, C, N), "first": first, "consts": consts,
        "woff": woff.reshape(P, TAPS, CB), "grid": grid.reshape(CB, PIX), "w2": w2.reshape(P, TAPS * CB),
        "w3": w3.reshape(P, C), "wq": wq.reshape(P, Q_COLS),
    }
    nc = bacc.Bacc("TRN2", target_bir_lowering=False, num_devices=1)
    args = [nc.dram_tensor(k, v.shape, F32, kind="ExternalInput").ap() for k, v in arrays.items()]
    out = nc.dram_tensor("out", (B, C, N), F32, kind="ExternalOutput").ap()
    build(nc, *args, out)
    r = run(nc, [arrays], core_ids=[0])
    return r.results[0]["out"].reshape(B, C, H, W)
```

```python
from contextlib import ExitStack

import concourse.bass as bass
from concourse import mybir

P = 128
B, C, H, W = 4, 256, 16, 16
HALVES = 2
B2 = B // HALVES
N = H * W
CB = 64
TAPS = 9
OFF = 3 * TAPS
OFF_ROWS = 32
CH = C // P
PIX = B2 * N
NQ = N // P
T = B2 * NQ
ROWS_Q = H // NQ
PER_SLOT = 3
TURNS = TAPS // PER_SLOT
TAPS_A = 5
BANK = 512
V_MAIN = BANK // CB
HP, WP = H + 2, W + 2
EPS = 1e-5
QMAX = float(2 ** 15 - 1)
LEAST_MAX = 1e-12
ROUND = 1.5 * 2.0 ** 23
SQRT2 = 1.4142135623730951
LEAST_POWER = 2.0 ** -14

F32 = mybir.dt.float32
BF16 = mybir.dt.bfloat16
I32 = mybir.dt.int32
U8 = mybir.dt.uint8
I8 = mybir.dt.int8
ALU = mybir.AluOpType
ACT = mybir.ActivationFunctionType
AX_X = mybir.AxisListType.X

(V_GN1S, V_GN1B, V_GN2S, V_GN2B, V_GN3S, V_GN3B, V_PEGB, V_BOFF, V_BNG, V_BNB, V_BNM, V_BNV) = (
    0, 1, 2, 3, 4, 6, 8, 9, 10, 14, 18, 22)
V_COLS = 26
Q_W1, Q_PEG, Q_W2, Q_W3 = 0, CH * CB, CH * CB + TAPS, CH * CB + TAPS + TAPS * CB
Q_COLS = Q_W3 + C
C_AVG2, C_DEV2, C_FOLD, C_COORD, C_ID = 0, P, 2 * P, 2 * P + CB, 2 * P + CB + H
C_AVG8, C_DEV8 = C_ID + P, C_ID + 2 * P
C_COLS = C_ID + 3 * P

IDLE = (7, 8, 4, 4, 4, 3, 5, 3, 4, 4)


def build(nc, x, first, consts, woff, grid, w2, w3, wq, out):
    with ExitStack() as ctx:
        def sb(name, shape, dt=F32):
            return ctx.enter_context(nc.sbuf_tensor(name, shape, dt))

        def ps(name, shape):
            return ctx.enter_context(nc.psum_tensor(name, shape, F32))

        def sem(name):
            return ctx.enter_context(nc.semaphore(name))

        x_sb = sb("x_sb", [P, CH, B2, HALVES, N])
        first_sb = sb("first_sb", [P, CH * CB + V_COLS])
        w1_sb = first_sb[:, 0:CH * CB].rearrange("p (c o) -> p c o", c=CH)
        vec = first_sb[:, CH * CB:CH * CB + V_COLS]
        consts_sb = sb("consts_sb", [P, C_COLS])
        ident = consts_sb[:, C_ID:C_ID + P]
        avg2 = consts_sb[:, C_AVG2:C_AVG2 + P]
        dev2 = consts_sb[:, C_DEV2:C_DEV2 + P]
        avg8 = consts_sb[:, C_AVG8:C_AVG8 + P]
        dev8 = consts_sb[:, C_DEV8:C_DEV8 + P]
        fold = consts_sb[:, C_FOLD:C_FOLD + CB]
        coord = consts_sb[:, C_COORD:C_COORD + H]
        woff_sb = sb("woff_sb", [P, TAPS, CB])
        grid_sb = sb("grid_sb", [CB, PIX])
        w2_sb = sb("w2_sb", [P, TAPS * CB])
        w3_sb = sb("w3_sb", [P, HALVES, C])
        wq_sb = sb("wq_sb", [P, Q_COLS])
        wq_mag = sb("wq_mag", [P, Q_COLS])
        wq_sign = sb("wq_sign", [P, Q_COLS])
        wqb = sb("wqb", [P, Q_COLS], BF16)
        w2q = sb("w2q", [P, TAPS, HALVES, CB], BF16)
        w3q = sb("w3q", [P, HALVES, C], BF16)
        pegq = sb("pegq", [P, TAPS, P], BF16)
        feat = sb("feat", [P, B2, HP, WP])
        feat_flat = sb("feat_flat", [P, PIX])
        om_sb = sb("om_sb", [P, PIX])
        omt_sb = sb("omt_sb", [P, B2, NQ, HALVES, OFF_ROWS])
        mask = sb("mask", [P, B2, NQ, HALVES, TAPS])
        hats = sb("hats", [P, T, HALVES, 2, TAPS, H])
        g_rows = [sb(f"g_rows{i}", [P, TAPS, H, W]) for i in range(3)]
        g_cols = [[sb(f"g_cols{b2}{h}", [P, TAPS * NQ, NQ, P]) for h in range(HALVES)] for b2 in range(B2)]
        v_sb = sb("v_sb", [P, B, NQ, TAPS, CB])
        feat2 = sb("feat2", [P, B2, N])
        y0 = sb("y0", [P, CH, B2, HALVES, N])
        act = sb("act", [P, B2, N])
        quot, res = (g_cols[0][h][:].rearrange("p k q n -> p (k q n)")[:, 0:CH * PIX * HALVES].rearrange(
            "p (c b h n) -> p c b h n", c=CH, b=B2, h=HALVES) for h in range(HALVES))
        n1_hi = sb("n1_hi", [P, CH, B2, HALVES, N], BF16)
        n1_lo = sb("n1_lo", [P, CH, B2, HALVES, N], BF16)
        pads = [sb(f"pad{i}", [P, B2, HP, WP], BF16) for i in range(4)]
        n4_hi = sb("n4_hi", [P, B2, N], BF16)
        n4_lo = sb("n4_lo", [P, B2, N], BF16)
        zeros = sb("zeros", [P, BANK], BF16)
        eps_sb = sb("eps_sb", [P, 1])
        stats = sb("stats", [P, B2, 4, 6])
        mv = sb("mv", [P, B2, 4, 2])
        var = sb("var", [P, B2, 4])
        dev_sb = sb("dev_sb", [P, B2, 4])
        std = sb("std", [P, B2, 4])
        rstd = sb("rstd", [P, B2, 4])
        gn_scale = sb("gn_scale", [P, B2, 4])
        gn_bias = sb("gn_bias", [P, B2, 4])
        bn_std = sb("bn_std", [P, 4])
        bn_inv = sb("bn_inv", [P, 4])
        bn_off = sb("bn_off", [P, 4])
        mx = sb("mx", [P, 12])
        q_inv = sb("q_inv", [P, 5])
        q_scale = sb("q_scale", [P, 5])
        q_floor = sb("q_floor", [P, 1])
        bn_mul = sb("bn_mul", [P, 4])

        slot = [ps(f"slot{i}", [P, 2 * BANK]) for i in range(3)]
        acc = [ps(f"acc{b2}", [P, BANK]) for b2 in range(B2)]
        small = [slot[2][:, BANK * b2:BANK * b2 + BANK] for b2 in range(B2)]

        first_in, consts_in, woff_in, grid_in, w2_in, w3_in, wq_in, stored = (
            sem(n) for n in ("first_in", "consts_in", "woff_in", "grid_in", "w2_in", "w3_in", "wq_in", "stored"))
        x_in = [[sem(f"x_in{b2}{c}") for c in range(CH)] for b2 in range(B2)]
        zeros_ready = sem("zeros_ready")
        pads_zero = sem("pads_zero")
        bn_var_ready = sem("bn_var_ready")
        bn_std_ready = sem("bn_std_ready")
        conv1_done = sem("conv1_done")
        mv_ready = sem("mv_ready")
        sums_done = sem("sums_done")
        sq_ready = sem("sq_ready")
        sq_done = sem("sq_done")
        var_ready = sem("var_ready")
        std_ready = sem("std_ready")
        gn_ready = sem("gn_ready")
        feat_ready = sem("feat_ready")
        flat_ready = sem("flat_ready")
        om_done = sem("om_done")
        om_ready = sem("om_ready")
        om_rest_ready = sem("om_rest_ready")
        omt_done = sem("omt_done")
        omt_ready = sem("omt_ready")
        mask_ready = sem("mask_ready")
        diff_ready = sem("diff_ready")
        abs_ready = sem("abs_ready")
        hats_made = sem("hats_made")
        hats_ready = sem("hats_ready")
        v_done = sem("v_done")
        v_ready = sem("v_ready")
        g_ready = sem("g_ready")
        turned = sem("turned")
        g_copied = sem("g_copied")
        sampled = sem("sampled")
        feat2_ready = sem("feat2_ready")
        conv3_done = sem("conv3_done")
        norm3_ready = sem("norm3_ready")
        sign_ready = sem("sign_ready")
        wq_ready = sem("wq_ready")
        placed = sem("placed")
        max_ready = sem("max_ready")
        max_spread = sem("max_spread")
        relu_ready = sem("relu_ready")
        quot_ready = sem("quot_ready")
        lo_ready = sem("lo_ready")
        hi_ready = sem("hi_ready")
        qconv_done = sem("qconv_done")
        bn_mul_ready = sem("bn_mul_ready")
        act_ready = sem("act_ready")
        sum_ready = sem("sum_ready")
        res_ready = sem("res_ready")
        chain = sem("dve_chain")

        block = ctx.enter_context(nc.Block())

        def window(tile, b2, k):
            dy, dx = k // 3, k % 3
            return tile[:, b2, dy:dy + H, dx:dx + W]

        def inner(tile, b2):
            return tile[:, b2, 1:1 + H, 1:1 + W]

        def image(t):
            return t.rearrange("p (y x) -> p y x", y=H)

        def rows(h):
            return slice(CB * h, CB * h + CB)

        def flat(t):
            return t.rearrange("p h n -> p (h n)")

        x_v = x.rearrange("(h b) (c p) n -> b c p h n", h=HALVES, c=CH)
        out_v = out.rearrange("(h b) (c p) n -> b c p h n", h=HALVES, c=CH)

        @block.sync
        def _(sp):
            sp.dma_start(first_sb[:], first).then_inc(first_in, 16)
            for b2 in range(B2):
                sp.dma_start(x_sb[:, 1, b2], x_v[b2, 1]).then_inc(x_in[b2][1], 16)
            sp.dma_start(woff_sb[:], woff).then_inc(woff_in, 16)
            sp.dma_start(wq_sb[:], wq).then_inc(wq_in, 16)
            sp.dma_start(w3_sb[:], w3).then_inc(w3_in, 16)
            for i in range(CH * B2):
                sp.wait_ge(res_ready, i + 1)
                sp.dma_start(out_v[i % B2, i // B2], res[:, i // B2, i % B2]).then_inc(stored, 16)
            sp.wait_ge(stored, 16 * CH * B2)

        @block.gpsimd
        def _(pool):
            nc.gpsimd.memset(feat[:], 0.0).then_inc(pads_zero, 1)
            for t in pads:
                nc.gpsimd.memset(t[:], 0.0).then_inc(pads_zero, 1)
            nc.gpsimd.memset(w2q[:], 0.0).then_inc(pads_zero, 1)
            nc.gpsimd.memset(w3q[:], 0.0).then_inc(pads_zero, 1)
            for b2 in range(B2):
                pool.wait_ge(feat_ready, b2 + 1)
                nc.gpsimd.tensor_copy(image(feat_flat[:, N * b2:N * b2 + N]), inner(feat, b2)).then_inc(flat_ready, 1)
            for t in range(T):
                pool.wait_ge(hats_made, t + 1)
                pool.wait_ge(mask_ready, t // NQ + 1)
                nc.gpsimd.tensor_tensor(hats[:, t, :, 1], hats[:, t, :, 1],
                                        mask[:, t // NQ, t % NQ].unsqueeze(3).to_broadcast([P, HALVES, TAPS, H]),
                                        ALU.mult).then_inc(hats_ready, 1)
            pool.wait_ge(consts_in, 16)
            pool.wait_ge(wq_ready, 1)
            nc.gpsimd.tensor_tensor(
                pegq[:], ident.unsqueeze(1).to_broadcast([P, TAPS, P]),
                wqb[:, Q_PEG:Q_PEG + TAPS].unsqueeze(2).to_broadcast([P, TAPS, P]), ALU.mult).then_inc(placed, 1)
            pool.wait_ge(pads_zero, 7)
            for h in range(HALVES):
                pool.wait_ge(placed, 2 * h + 1)
                nc.gpsimd.tensor_copy(w2q[rows(h), :, h, :],
                                      wqb[rows(h), Q_W2:Q_W2 + TAPS * CB].rearrange("p (k o) -> p k o", k=TAPS)
                                      ).then_inc(placed, 1)
                nc.gpsimd.tensor_copy(w3q[rows(h), h, :], wqb[rows(h), Q_W3:Q_W3 + C]).then_inc(placed, 1)

        @block.tensor
        def _(pe):
            def idle(n, bank):
                for _ in range(n):
                    nc.tensor.matmul(bank, zeros[:, 0:P], zeros[:], start=True, stop=True)

            spare = slot[1][:, BANK:2 * BANK]

            pe.wait_ge(zeros_ready, 1)
            idle(IDLE[0], spare)
            pe.wait_ge(first_in, 16)
            for b2 in range(B2):
                for c in range(CH):
                    pe.wait_ge(x_in[b2][c], 16)
                    for h in range(HALVES):
                        mm = nc.tensor.matmul(acc[b2][rows(h), 0:N], w1_sb[:, c, :], x_sb[:, c, b2, h, :],
                                              start=(c == 0), stop=(c == CH - 1))
                mm.then_inc(conv1_done, 1)

            def pair_sums(n, b2):
                pe.wait_ge(mv_ready, n)
                nc.tensor.matmul(small[b2][:, 0:2], avg2, mv[:, b2, 0, :], start=True, stop=True)
                nc.tensor.matmul(small[b2][:, 4:5], dev2, mv[:, b2, 0, 0:1], start=True, stop=True
                                 ).then_inc(sums_done, 1)

            pe.wait_ge(consts_in, 16)
            pair_sums(1, 0)
            pair_sums(2, 1)
            idle(IDLE[1], spare)

            def om_step(b2, s):
                for p in range(2):
                    k = s + TAPS_A * p
                    if k < TAPS:
                        mm = nc.tensor.matmul(slot[0][CB * p:CB * p + CB, BANK * b2:BANK * b2 + N],
                                              woff_sb[:, k, :], window(feat, b2, k), start=(s == 0),
                                              stop=(k in (TAPS_A - 1, TAPS - 1)))
                return mm

            def om_turn(b2):
                pe.wait_ge(om_ready, b2 + 1)
                pe.wait_ge(om_rest_ready, b2 + 1)
                for q in range(NQ):
                    at = N * b2 + P * q
                    mm = nc.tensor.matmul(slot[1][:, BANK * b2 + CB * q:BANK * b2 + CB * q + CB],
                                          om_sb[:, at:at + P], fold, start=True, stop=True)
                mm.then_inc(omt_done, 1)

            pe.wait_ge(woff_in, 16)
            for b2 in range(B2):
                pe.wait_ge(feat_ready, b2 + 1)
                for s in range(TAPS_A):
                    mm = om_step(b2, s)
                    if b2 == 1 and s == 2:
                        om_turn(0)
                mm.then_inc(om_done, 1)

            v_banks = [small[0], small[1], acc[0][:], acc[1][:]]
            pe.wait_ge(w2_in, 16)

            def make_v(i):
                b2, q, h = i // 4, i // 2 % 2, i % 2
                pe.wait_ge(flat_ready, b2 + 1)
                if i >= 4:
                    pe.wait_ge(v_ready, i - 3)
                at = N * b2 + P * q
                lhs = feat_flat[rows(h), at:at + P]
                nc.tensor.matmul(v_banks[i % 4], lhs, w2_sb[rows(h), 0:BANK], start=True, stop=True
                                 ).then_inc(v_done, 1)

            def make_last_v(i):
                b2, q, h = i // 4, i // 2 % 2, i % 2
                at = BANK * h + CB * (i // 2)
                return nc.tensor.matmul(slot[0][:, at:at + CB], feat_flat[rows(h), N * b2 + P * q:N * b2 + P * q + P],
                                        w2_sb[rows(h), BANK:TAPS * CB], start=True, stop=True)

            make_v(0)
            make_v(1)
            om_turn(1)
            make_last_v(0)
            make_last_v(1)
            for i in range(2, 2 * T):
                make_v(i)
                mm = make_last_v(i)
            mm.then_inc(v_done, 1)

            def turn(i):
                pe.wait_ge(g_ready, i + 1)
                for j in range(TURNS):
                    if i == 0:
                        pe.wait_ge(v_ready, 2 * T + 1)
                    else:
                        pe.wait_ge(g_copied, TURNS * (i - 1) + j + 1)
                    for k in range(PER_SLOT * j, PER_SLOT * j + PER_SLOT):
                        for q in range(NQ):
                            at = P * (NQ * (k - PER_SLOT * j) + q)
                            mm = nc.tensor.transpose(slot[j][:, at:at + P],
                                                     g_rows[i % 3][:, k, ROWS_Q * q:ROWS_Q * q + ROWS_Q, :], ident)
                    mm.then_inc(turned, 1)

            def sample(b2, j):
                pe.wait_ge(g_copied, TURNS * (4 * b2 + 3) + j + 1)
                for k in range(PER_SLOT * j, PER_SLOT * j + PER_SLOT):
                    for q in range(NQ):
                        for h in range(HALVES):
                            mm = nc.tensor.matmul(
                                acc[b2][rows(h), 0:N], v_sb[:, B2 * h + b2, q, k, :],
                                g_cols[b2][h][:, NQ * k + q].rearrange("p a n -> p (a n)"),
                                start=(k == 0 and q == 0), stop=(k == TAPS - 1 and q == NQ - 1))
                return mm

            for i in range(5):
                turn(i)
            sample(0, 0)
            turn(5)
            sample(0, 1)
            turn(6)
            sample(0, 2).then_inc(sampled, 1)
            turn(7)

            def conv3(b2):
                pe.wait_ge(feat2_ready, b2 + 1)
                for c in range(CH):
                    for h in range(HALVES):
                        mm = nc.tensor.matmul(slot[c][:, BANK * b2 + N * h:BANK * b2 + N * h + N],
                                              w3_sb[:, h, P * c:P * c + P], feat2[:, b2, :],
                                              start=True, stop=True)
                    mm.then_inc(conv3_done, 1)

            def eight_means(b2):
                pe.wait_ge(mv_ready, 4 + 2 * b2)
                nc.tensor.matmul(small[b2][:, 8:12], avg8, mv[:, b2, :, 0], start=True, stop=True)
                nc.tensor.matmul(small[b2][:, 12:16], dev8, mv[:, b2, :, 0], start=True, stop=True
                                 ).then_inc(sums_done, 1)

            def eight_vars(b2):
                pe.wait_ge(sq_ready, b2 + 1)
                nc.tensor.matmul(small[b2][:, 16:20], avg8, var[:, b2, :], start=True, stop=True
                                 ).then_inc(sq_done, 1)

            sample(1, 0)
            pe.wait_ge(g_copied, TURNS * 2 * T)
            pair_sums(3, 0)
            sample(1, 1)
            pe.wait_ge(w3_in, 16)
            conv3(0)
            sample(1, 2).then_inc(sampled, 1)
            eight_means(0)
            idle(IDLE[2], spare)
            pair_sums(5, 1)
            eight_vars(0)
            idle(IDLE[3], spare)
            conv3(1)
            idle(IDLE[4], acc[0][:])
            eight_means(1)
            eight_vars(1)
            idle(IDLE[5], acc[0][:])

            def spread_max(n, first_col, cols):
                for i in range(cols):
                    pe.wait_ge(max_ready, n + i)
                    mm = nc.tensor.transpose(small[0][:, 128 + P * i:128 + P * i + P],
                                             mx[:, first_col + i:first_col + i + 1].to_broadcast([P, P]), ident)
                mm.then_inc(max_spread, 1)

            spread_max(1, 4, 1)
            idle(IDLE[6], spare)
            pe.wait_ge(placed, 1 + 2 * HALVES)
            for b2 in range(B2):
                for part, ready in ((n1_lo, lo_ready), (n1_hi, hi_ready)):
                    for c in range(CH):
                        pe.wait_ge(ready, CH * b2 + c + 1)
                        for h in range(HALVES):
                            mm = nc.tensor.matmul(acc[b2][rows(h), 0:N], wqb[:, Q_W1 + CB * c:Q_W1 + CB * c + CB],
                                                  part[:, c, b2, h, :], start=(part is n1_lo and c == 0),
                                                  stop=(part is n1_hi and c == CH - 1))
                mm.then_inc(qconv_done, 1)
            spread_max(2, 5, 2)
            idle(IDLE[7], spare)

            def window_conv(weights, lo, hi, n):
                for b2 in range(B2):
                    for part, ready in ((lo, lo_ready), (hi, hi_ready)):
                        pe.wait_ge(ready, CH * B2 + B2 * (n - 2) + b2 + 1)
                        for k in range(TAPS):
                            mm = nc.tensor.matmul(acc[b2][:, 0:N], weights(k), window(part, b2, k),
                                                  start=(part is lo and k == 0), stop=(part is hi and k == TAPS - 1))
                    mm.then_inc(qconv_done, 1)

            window_conv(lambda k: pegq[:, k, :], pads[0], pads[1], 2)
            idle(IDLE[8], spare)
            spread_max(4, 7, 2)
            idle(IDLE[9], spare)
            window_conv(lambda k: w2q[:, k].rearrange("p h o -> p (h o)"), pads[2], pads[3], 3)
            idle(IDLE[8], spare)
            spread_max(6, 9, 2)
            idle(IDLE[9], spare)
            for c in range(CH):
                for b2 in range(B2):
                    for part, ready in ((n4_lo, lo_ready), (n4_hi, hi_ready)):
                        pe.wait_ge(ready, CH * B2 + B2 * 2 + b2 + 1)
                        for h in range(HALVES):
                            mm = nc.tensor.matmul(slot[c][:, BANK * b2 + N * h:BANK * b2 + N * h + N],
                                                  w3q[:, h, P * c:P * c + P], part[:, b2, :],
                                                  start=(part is n4_lo and h == 0), stop=(part is n4_hi),
                                                  skip_group_check=True)
                    mm.then_inc(qconv_done, 1)

        @block.scalar
        def _(a):
            for b2 in range(B2):
                a.dma_start(x_sb[:, 0, b2], x_v[b2, 0]).then_inc(x_in[b2][0], 16)
            a.dma_start(consts_sb[:], consts).then_inc(consts_in, 16)
            a.dma_start(grid_sb[:], grid).then_inc(grid_in, 16)
            a.dma_start(w2_sb[:], w2).then_inc(w2_in, 16)
            a.wait_ge(bn_var_ready, 1)
            nc.scalar.activation(bn_std[:], bn_std[:], ACT.Sqrt).then_inc(bn_std_ready, 1)

            def root(done, b2, n):
                a.wait_ge(var_ready, done)
                nc.scalar.activation(std[:, b2, 0:n], var[:, b2, 0:n], ACT.Sqrt, bias=eps_sb[:, 0:1]
                                     ).then_inc(std_ready, 1)

            def normalise(done, b2, dst, src, ready):
                a.wait_ge(gn_ready, done)
                nc.scalar.activation(dst, src, ACT.Relu, bias=gn_bias[:, b2, 0:1], scale=gn_scale[:, b2, 0:1]
                                     ).then_inc(ready, 1)

            root(1, 0, 1)
            a.wait_ge(pads_zero, 1)
            normalise(1, 0, inner(feat, 0), image(acc[0][:, 0:N]), feat_ready)
            root(2, 1, 1)
            normalise(2, 1, inner(feat, 1), image(acc[1][:, 0:N]), feat_ready)
            nc.scalar.preload_act_table(ACT.Sigmoid)
            a.wait_ge(wq_in, 16)
            nc.scalar.activation(wq_sign[:], wq_sb[:], ACT.Sign).then_inc(sign_ready, 1)

            def copy_om_rest(b2):
                a.wait_ge(om_done, b2 + 1)
                nc.scalar.activation(om_sb[CB:P, N * b2:N * b2 + N], slot[0][CB:P, BANK * b2:BANK * b2 + N],
                                     ACT.Copy).then_inc(om_rest_ready, 1)

            def copy_omt(b2):
                a.wait_ge(omt_done, b2 + 1)
                nc.scalar.activation(omt_sb[:, b2].rearrange("p q h o -> p (q h o)"),
                                     slot[1][:, BANK * b2:BANK * b2 + NQ * CB], ACT.Copy).then_inc(omt_ready, 1)
                a.wait_ge(omt_ready, b2 + 1)
                nc.scalar.activation(mask[:, b2], omt_sb[:, b2, :, :, 2 * TAPS:OFF], ACT.Sigmoid
                                     ).then_inc(mask_ready, 1)

            def distance(t):
                a.wait_ge(diff_ready, t + 1)
                v = hats[:, t].rearrange("p h a k y -> p (h a k y)")
                nc.scalar.activation(v, v, ACT.Abs).then_inc(abs_ready, 1)

            v_banks = [small[0], small[1], acc[0][:], acc[1][:]]

            def copy_v(i):
                b2, q, h = i // 4, i // 2 % 2, i % 2
                a.wait_ge(v_done, i + 1)
                nc.scalar.activation(v_sb[:, B2 * h + b2, q, 0:V_MAIN, :].rearrange("p k o -> p (k o)"),
                                     v_banks[i % 4], ACT.Copy).then_inc(v_ready, 1)

            copy_om_rest(0)
            copy_omt(0)
            distance(0)
            copy_om_rest(1)
            distance(1)
            copy_v(0)
            copy_v(1)
            copy_omt(1)
            copy_v(2)
            distance(2)
            copy_v(3)
            distance(3)
            for i in range(4, 2 * T):
                copy_v(i)
            a.wait_ge(v_done, 2 * T + 1)
            for h in range(HALVES):
                last = nc.scalar.activation(v_sb[:, B2 * h:B2 * h + B2, :, V_MAIN, :],
                                            slot[0][:, BANK * h:BANK * h + T * CB].rearrange(
                                                "p (b q o) -> p b q o", b=B2, q=NQ), ACT.Copy)
            last.then_inc(v_ready, 1)

            def copy_g(i):
                t, h = i // HALVES, i % HALVES
                for j in range(TURNS):
                    a.wait_ge(turned, TURNS * i + j + 1)
                    per = PER_SLOT * NQ
                    nc.scalar.activation(g_cols[t // NQ][h][:, per * j:per * j + per, t % NQ, :],
                                         slot[j][:, 0:per * P].rearrange("p (k n) -> p k n", k=per),
                                         ACT.Copy).then_inc(g_copied, 1)

            for i in range(2 * T):
                copy_g(i)
            nc.scalar.preload_act_table(ACT.Sqrt)
            root(3, 0, 1)
            normalise(3, 0, feat2[:, 0, :], acc[0][:, 0:N], feat2_ready)

            def norm3(b2):
                a.wait_ge(gn_ready, 5 + b2)
                for h in range(HALVES):
                    nc.scalar.activation(y0[:, 0, b2, h, :], slot[0][:, BANK * b2 + N * h:BANK * b2 + N * h + N],
                                         ACT.Identity, bias=gn_bias[:, b2, h:h + 1], scale=gn_scale[:, b2, h:h + 1]
                                         ).then_inc(norm3_ready, 1)

            root(4, 1, 1)
            normalise(4, 1, feat2[:, 1, :], acc[1][:, 0:N], feat2_ready)
            root(5, 0, 4)
            norm3(0)
            root(6, 1, 4)
            norm3(1)
            for b2 in range(B2):
                a.wait_ge(sum_ready, CH * b2 + CH)
                nc.scalar.activation(flat(y0[:, 0, b2]), flat(y0[:, 0, b2]), ACT.Relu).then_inc(relu_ready, 1)

            def high_part(dst, src, done):
                a.wait_ge(quot_ready, done)
                nc.scalar.activation(dst, src, ACT.Copy, scale=256.0).then_inc(hi_ready, 1)

            def byte(t, n, dt):
                return t.bitcast(dt).rearrange("p (n e) -> p n e", e=4)[:, :, n]

            for b2 in range(B2):
                for c in range(CH):
                    high_part(flat(n1_hi[:, c, b2]), byte(flat(quot[:, c, b2]), 1, I8), CH * b2 + c + 1)
            q2 = quot[:, 0, 0].rearrange("p b n -> p (b n)")
            a.wait_ge(pads_zero, 5)
            for n, hi in ((2, pads[1]), (3, pads[3])):
                for b2 in range(B2):
                    high_part(inner(hi, b2), image(byte(q2[:, N * b2:N * b2 + N], 1, I8)),
                              CH * B2 + B2 * (n - 2) + b2 + 1)
                for b2 in range(B2):
                    a.wait_ge(bn_mul_ready, n - 1)
                    a.wait_ge(qconv_done, B2 * (n - 1) + b2 + 1)
                    nc.scalar.activation(act[:, b2, :], acc[b2][:, 0:N], ACT.Relu, bias=bn_off[:, n - 2:n - 1],
                                         scale=bn_mul[:, n - 2:n - 1]).then_inc(act_ready, 1)
            for b2 in range(B2):
                high_part(n4_hi[:, b2, :], byte(q2[:, N * b2:N * b2 + N], 1, I8), CH * B2 + B2 * 2 + b2 + 1)
            for i in range(CH * B2):
                c, b2 = i // B2, i % B2
                a.wait_ge(sum_ready, CH * B2 + i + 1)
                nc.scalar.activation(flat(res[:, c, b2]), flat(res[:, c, b2]), ACT.Relu, bias=bn_off[:, 2 + c:3 + c]
                                     ).then_inc(res_ready, 1)

        @block.vector
        def _(dve):
            count = [0]

            def settle(ins):
                count[0] += 1
                ins.then_inc(chain, 1)
                dve.wait_ge(chain, count[0])

            tt, ts, stt = nc.vector.tensor_tensor, nc.vector.tensor_scalar, nc.vector.scalar_tensor_tensor
            nc.vector.memset(zeros[:], 0.0).then_inc(zeros_ready, 1)
            nc.vector.memset(eps_sb[:], EPS)
            dve.wait_ge(first_in, 16)
            ts(bn_std[:], vec[:, V_BNV:V_BNV + 4], EPS, None, ALU.add).then_inc(bn_var_ready, 1)
            dve.wait_ge(bn_std_ready, 1)
            settle(nc.vector.reciprocal(bn_std[:], bn_std[:]))
            settle(tt(bn_inv[:], bn_std[:], vec[:, V_BNG:V_BNG + 4], ALU.mult))
            settle(tt(bn_off[:], bn_inv[:], vec[:, V_BNM:V_BNM + 4], ALU.mult))
            settle(tt(bn_off[:], vec[:, V_BNB:V_BNB + 4], bn_off[:], ALU.subtract))
            settle(stt(bn_off[:, 0:1], bn_inv[:, 0:1], vec[:, V_PEGB:V_PEGB + 1], bn_off[:, 0:1], ALU.mult, ALU.add))

            def moments(b2, srcs):
                for i, src in enumerate(srcs):
                    last = nc.vector.bn_stats(stats[:, b2, i, :], src)
                settle(last)
                for i in range(len(srcs)):
                    last = nc.vector.bn_aggr(mv[:, b2, i, :], stats[:, b2, i, :])
                last.then_inc(mv_ready, 1)

            def pair_var(done, b2):
                dve.wait_ge(sums_done, done)
                ts(var[:, b2, 0:1], small[b2][:, 4:5], small[b2][:, 4:5], small[b2][:, 1:2], ALU.mult, ALU.add
                   ).then_inc(var_ready, 1)

            def pair_scale(done, b2, gamma, beta):
                dve.wait_ge(std_ready, done)
                settle(nc.vector.reciprocal(rstd[:, b2, 0:1], std[:, b2, 0:1]))
                settle(tt(gn_scale[:, b2, 0:1], rstd[:, b2, 0:1], vec[:, gamma:gamma + 1], ALU.mult))
                stt(gn_bias[:, b2, 0:1], gn_scale[:, b2, 0:1], small[b2][:, 0:1], vec[:, beta:beta + 1], ALU.mult,
                    ALU.subtract, reverse1=True).then_inc(gn_ready, 1)

            dve.wait_ge(conv1_done, 1)
            moments(0, [acc[0][:, 0:N]])
            pair_var(1, 0)
            dve.wait_ge(conv1_done, 2)
            moments(1, [acc[1][:, 0:N]])
            pair_scale(1, 0, V_GN1S, V_GN1B)
            pair_var(2, 1)
            pair_scale(2, 1, V_GN1S, V_GN1B)

            dve.wait_ge(wq_in, 16)
            settle(ts(wq_mag[:].bitcast(I32), wq_sb[:].bitcast(I32), 0x7FFFFFFF, None, ALU.bitwise_and))
            settle(ts(wq_mag[:], wq_mag[:], 1e-20, SQRT2, ALU.add, ALU.mult))
            settle(ts(wq_mag[:].bitcast(I32), wq_mag[:].bitcast(I32), 0x7F800000, None, ALU.bitwise_and))

            def add_grid(b2):
                dve.wait_ge(om_done, b2 + 1)
                stt(om_sb[0:CB, N * b2:N * b2 + N], slot[0][0:CB, BANK * b2:BANK * b2 + N],
                    vec[0:CB, V_BOFF:V_BOFF + 1], grid_sb[:, N * b2:N * b2 + N], ALU.add, ALU.add
                    ).then_inc(om_ready, 1)

            def differences(t):
                dve.wait_ge(omt_ready, t // NQ + 1)
                tt(hats[:, t].rearrange("p h a k y -> p h (a k) y"),
                   omt_sb[:, t // NQ, t % NQ, :, 0:2 * TAPS].unsqueeze(3).to_broadcast([P, HALVES, 2 * TAPS, H]),
                   coord.unsqueeze(1).unsqueeze(1).to_broadcast([P, HALVES, 2 * TAPS, H]),
                   ALU.subtract).then_inc(diff_ready, 1)

            def make_hats(t):
                dve.wait_ge(abs_ready, t + 1)
                v = hats[:, t].rearrange("p h a k y -> p (h a k y)")
                ts(v, v, 1.0, 1.0, ALU.min, ALU.subtract).then_inc(hats_made, 1)

            def make_g(i):
                t, h = i // HALVES, i % HALVES
                dve.wait_ge(hats_ready, t + 1)
                if i >= 3:
                    dve.wait_ge(turned, TURNS * (i - 2))
                tt(g_rows[i % 3][:], hats[:, t, h, 1].unsqueeze(3).to_broadcast([P, TAPS, H, W]),
                   hats[:, t, h, 0].unsqueeze(2).to_broadcast([P, TAPS, H, W]), ALU.mult).then_inc(g_ready, 1)

            dve.wait_ge(grid_in, 16)
            add_grid(0)
            settle(ts(wq_mag[:], wq_mag[:], LEAST_POWER, 1.0, ALU.max, ALU.min))
            differences(0)
            differences(1)
            add_grid(1)
            make_hats(0)
            make_hats(1)
            make_g(0)
            differences(2)
            differences(3)
            make_g(1)
            make_hats(2)
            make_hats(3)
            make_g(2)
            dve.wait_ge(sign_ready, 1)
            tt(wqb[:], wq_mag[:], wq_sign[:], ALU.mult).then_inc(wq_ready, 1)
            for i in range(3, 2 * T):
                make_g(i)

            def eight_moments(b2):
                dve.wait_ge(conv3_done, CH * b2 + CH)
                moments(b2, [slot[c][:, BANK * b2 + N * h:BANK * b2 + N * h + N]
                             for c in range(CH) for h in range(HALVES)])

            def eight_squares(b2):
                dve.wait_ge(sums_done, 4 + 2 * b2)
                settle(nc.vector.tensor_copy(dev_sb[:, b2, :], small[b2][:, 12:16]))
                settle(tt(dev_sb[:, b2, :], dev_sb[:, b2, :], dev_sb[:, b2, :], ALU.mult))
                tt(var[:, b2, :], dev_sb[:, b2, :], mv[:, b2, :, 1], ALU.add).then_inc(sq_ready, 1)

            def eight_var(b2):
                dve.wait_ge(sq_done, b2 + 1)
                nc.vector.tensor_copy(var[:, b2, :], small[b2][:, 16:20]).then_inc(var_ready, 1)

            def eight_scale(b2):
                dve.wait_ge(std_ready, 5 + b2)
                settle(nc.vector.reciprocal(rstd[:, b2, :], std[:, b2, :]))
                for c in range(CH):
                    last = ts(gn_scale[:, b2, HALVES * c:HALVES * c + HALVES],
                              rstd[:, b2, HALVES * c:HALVES * c + HALVES], vec[:, V_GN3S + c:V_GN3S + c + 1], None,
                              ALU.mult)
                settle(last)
                settle(tt(dev_sb[:, b2, :], gn_scale[:, b2, :], small[b2][:, 8:12], ALU.mult))
                for c in range(CH):
                    last = ts(gn_bias[:, b2, HALVES * c:HALVES * c + HALVES],
                              dev_sb[:, b2, HALVES * c:HALVES * c + HALVES], -1.0, vec[:, V_GN3B + c:V_GN3B + c + 1],
                              ALU.mult, ALU.add)
                last.then_inc(gn_ready, 1)

            def residual(b2):
                dve.wait_ge(gn_ready, 5 + b2)
                for h in range(HALVES):
                    last = ts(y0[:, 1, b2, h, :], slot[1][:, BANK * b2 + N * h:BANK * b2 + N * h + N],
                              gn_scale[:, b2, HALVES + h:HALVES + h + 1], gn_bias[:, b2, HALVES + h:HALVES + h + 1],
                              ALU.mult, ALU.add)
                settle(last)
                for c in (1, 0):
                    if c == 0:
                        dve.wait_ge(norm3_ready, HALVES * (b2 + 1))
                    last = nc.vector.tensor_tensor_reduce(flat(y0[:, c, b2]), flat(y0[:, c, b2]), flat(x_sb[:, c, b2]),
                                                          1.0, 0.0, ALU.add, ALU.max, mx[:, 2 * b2 + c:2 * b2 + c + 1])
                    last.then_inc(sum_ready, 1)

            dve.wait_ge(sampled, 1)
            moments(0, [acc[0][:, 0:N]])
            pair_var(3, 0)
            pair_scale(3, 0, V_GN2S, V_GN2B)
            eight_moments(0)
            dve.wait_ge(sampled, 2)
            moments(1, [acc[1][:, 0:N]])
            pair_var(5, 1)
            pair_scale(4, 1, V_GN2S, V_GN2B)
            eight_squares(0)
            eight_var(0)
            eight_scale(0)
            residual(0)
            eight_moments(1)
            eight_squares(1)
            eight_var(1)
            eight_scale(1)
            residual(1)
            dve.wait_ge(sum_ready, CH * B2)
            nc.vector.tensor_reduce(mx[:, 4:5], mx[:, 0:4], AX_X, ALU.max).then_inc(max_ready, 1)
            for b2 in range(B2):
                last = ts(flat(y0[:, 1, b2]), flat(y0[:, 1, b2]), 0.0, None, ALU.max)
            settle(last)

            def scale_of(n, cols, floor):
                dve.wait_ge(max_spread, n)
                settle(nc.vector.tensor_reduce(q_scale[:, n:n + 1], small[0][:, 128:128 + P * cols], AX_X, ALU.max))
                settle(ts(q_scale[:, n:n + 1], q_scale[:, n:n + 1], floor, 1.0 / QMAX, ALU.max, ALU.mult))
                settle(nc.vector.reciprocal(q_inv[:, n:n + 1], q_scale[:, n:n + 1]))

            def quotient(n, dst, src):
                ts(dst, src, q_inv[:, n:n + 1], ROUND, ALU.mult, ALU.add).then_inc(quot_ready, 1)

            def byte(t, n, dt):
                return t.bitcast(dt).rearrange("p (n e) -> p n e", e=4)[:, :, n]

            def low_part(dst, src, done):
                dve.wait_ge(quot_ready, done)
                nc.vector.tensor_copy(dst, src).then_inc(lo_ready, 1)

            scale_of(1, 1, LEAST_MAX)
            for b2 in range(B2):
                for c in range(CH):
                    if c == 0:
                        dve.wait_ge(relu_ready, b2 + 1)
                    quotient(1, flat(quot[:, c, b2]), flat(y0[:, c, b2]))
                    low_part(flat(n1_lo[:, c, b2]), byte(flat(quot[:, c, b2]), 0, U8), CH * b2 + c + 1)
            ts(q_floor[:], q_inv[:, 1:2], LEAST_MAX, None, ALU.mult)

            q2 = quot[:, 0, 0].rearrange("p b n -> p (b n)")

            def parts(n, srcs, lo):
                for b2 in range(B2):
                    if b2 == 0:
                        dve.wait_ge(hi_ready, CH * B2 + B2 * (n - 2))
                        dve.wait_ge(lo_ready, CH * B2 + B2 * (n - 2))
                    at = N * b2
                    quotient(n, q2[:, at:at + N], srcs[b2])
                    low = byte(q2[:, at:at + N], 0, U8)
                    low_part(inner(lo, b2) if lo is not n4_lo else lo[:, b2, :],
                             image(low) if lo is not n4_lo else low, CH * B2 + B2 * (n - 2) + b2 + 1)

            for b2 in range(B2):
                dve.wait_ge(qconv_done, b2 + 1)
                nc.vector.tensor_reduce(mx[:, 5 + b2:6 + b2], acc[b2][:, 0:N], AX_X, ALU.max,
                                        apply_absolute_value=True).then_inc(max_ready, 1)
            scale_of(2, 2, q_floor[:, 0:1])
            parts(2, [acc[b2][:, 0:N] for b2 in range(B2)], pads[0])
            settle(tt(q_scale[:, 2:3], q_scale[:, 2:3], q_scale[:, 1:2], ALU.mult))
            tt(bn_mul[:, 0:1], q_scale[:, 2:3], bn_inv[:, 0:1], ALU.mult).then_inc(bn_mul_ready, 1)
            for n, lo in ((3, pads[2]), (4, n4_lo)):
                for b2 in range(B2):
                    dve.wait_ge(act_ready, B2 * (n - 3) + b2 + 1)
                    at = 7 + B2 * (n - 3) + b2
                    nc.vector.tensor_reduce(mx[:, at:at + 1], act[:, b2, :], AX_X, ALU.max).then_inc(max_ready, 1)
                scale_of(n, 2, LEAST_MAX)
                parts(n, [act[:, b2, :] for b2 in range(B2)], lo)
                if n == 3:
                    tt(bn_mul[:, 1:2], q_scale[:, 3:4], bn_inv[:, 1:2], ALU.mult).then_inc(bn_mul_ready, 1)
            settle(ts(bn_mul[:, 2:4], bn_inv[:, 2:4], q_scale[:, 4:5], None, ALU.mult))
            for i in range(CH * B2):
                c, b2 = i // B2, i % B2
                dve.wait_ge(qconv_done, 3 * B2 + i + 1)
                stt(flat(res[:, c, b2]), slot[c][:, BANK * b2:BANK * b2 + BANK], bn_mul[:, 2 + c:3 + c],
                    flat(y0[:, c, b2]), ALU.mult, ALU.add).then_inc(sum_ready, 1)


def kernel(**inputs):
    import numpy as np
    import concourse.bacc as bacc
    from concourse.bass_utils import run_bass_kernel_spmd as run

    f = np.float32
    a = {k: np.asarray(v) for k, v in inputs.items()}

    first = np.zeros((P, CH * CB + V_COLS), f)
    first[:, 0:CH * CB] = a["L0_conv_w1"][:, :, 0, 0].reshape(CB, CH, P).transpose(2, 1, 0).reshape(P, CH * CB)
    vec = first[:, CH * CB:]

    def both(col, v):
        vec[:CB, col] = v
        vec[CB:, col] = v

    for col, name in ((V_GN1S, "L0_conv_gn1_scale"), (V_GN1B, "L0_conv_gn1_bias"), (V_GN2S, "L0_conv_gn2_scale"),
                      (V_GN2B, "L0_conv_gn2_bias"), (V_PEGB, "L1_conv_peg_b")):
        both(col, a[name])
    for col, name in ((V_GN3S, "L0_conv_gn3_scale"), (V_GN3B, "L0_conv_gn3_bias")):
        vec[:, col:col + CH] = a[name].reshape(CH, P).T
    for h in range(HALVES):
        vec[OFF_ROWS * h:OFF_ROWS * h + OFF, V_BOFF] = a["L0_conv_b_off"]
    for col, p in ((V_BNG, "g"), (V_BNB, "b"), (V_BNM, "m"), (V_BNV, "v")):
        both(col, a["L1_conv_bn1_" + p])
        both(col + 1, a["L1_conv_bn2_" + p])
        vec[:, col + 2:col + 4] = a["L1_conv_bn3_" + p].reshape(CH, P).T

    consts = np.zeros((P, C_COLS), f)
    eye = np.eye(P, dtype=f)
    consts[:, C_ID:C_ID + P] = eye
    for g, at_avg, at_dev in ((2, C_AVG2, C_DEV2), (8, C_AVG8, C_DEV8)):
        mean = np.kron(np.eye(P // g, dtype=f), np.full((g, g), 1.0 / g, f))
        consts[:, at_avg:at_avg + P] = mean
        consts[:, at_dev:at_dev + P] = eye - mean
    for p in range(2):
        consts[CB * p:CB * p + CB, C_FOLD:C_FOLD + CB] = eye[0:CB, 0:CB]
    consts[:, C_COORD:C_COORD + H] = np.arange(H, dtype=f)

    woff = np.zeros((HALVES, CB, TAPS, HALVES, OFF_ROWS), f)
    for h in range(HALVES):
        woff[h, :, :, h, 0:OFF] = a["L0_conv_w_off"].reshape(OFF, CB, TAPS).transpose(1, 2, 0)
    grid = np.zeros((HALVES, OFF_ROWS, B2, H, W), f)
    for k in range(TAPS):
        grid[:, k] = np.arange(W, dtype=f) + (k % 3 - 1)
        grid[:, TAPS + k] = (np.arange(H, dtype=f) + (k // 3 - 1))[:, None]
    w2 = np.zeros((HALVES, CB, TAPS * CB), f)
    w2[:] = a["L0_conv_w2"].reshape(CB, CB, TAPS).transpose(1, 2, 0).reshape(CB, TAPS * CB)
    w3 = np.zeros((HALVES, CB, HALVES, C), f)
    for h in range(HALVES):
        w3[h, :, h] = a["L0_conv_w3"][:, :, 0, 0].T
    wq = np.zeros((HALVES, CB, Q_COLS), f)
    wq.reshape(P, Q_COLS)[:, Q_W1:Q_W1 + CH * CB] = a["L1_conv_w1"][:, :, 0, 0].reshape(CB, CH, P).transpose(
        2, 1, 0).reshape(P, CH * CB)
    wq[:, :, Q_PEG:Q_PEG + TAPS] = a["L1_conv_peg_w"].reshape(CB, TAPS)
    wq[:, :, Q_W2:Q_W2 + TAPS * CB] = a["L1_conv_w2"].reshape(CB, CB, TAPS).transpose(1, 2, 0).reshape(CB, TAPS * CB)
    wq[:, :, Q_W3:Q_W3 + C] = a["L1_conv_w3"][:, :, 0, 0].T

    arrays = {
        "x": np.ascontiguousarray(a["x"]).reshape(B, C, N), "first": first, "consts": consts,
        "woff": woff.reshape(P, TAPS, CB), "grid": grid.reshape(CB, PIX), "w2": w2.reshape(P, TAPS * CB),
        "w3": w3.reshape(P, HALVES, C), "wq": wq.reshape(P, Q_COLS),
    }
    nc = bacc.Bacc("TRN2", target_bir_lowering=False, num_devices=1)
    args = [nc.dram_tensor(k, v.shape, F32, kind="ExternalInput").ap() for k, v in arrays.items()]
    out = nc.dram_tensor("out", (B, C, N), F32, kind="ExternalOutput").ap()
    build(nc, *args, out)
    r = run(nc, [arrays], core_ids=[0])
    return r.results[0]["out"].reshape(B, C, H, W)
```

```python
from contextlib import ExitStack

import concourse.bass as bass
from concourse import mybir

P = 128
B, C, H, W = 4, 256, 16, 16
HALVES = 2
B2 = B // HALVES
N = H * W
CB = 64
TAPS = 9
OFF = 3 * TAPS
OFF_ROWS = 32
CH = C // P
PIX = B2 * N
NQ = N // P
T = B2 * NQ
ROWS_Q = H // NQ
PER_SLOT = 3
TURNS = TAPS // PER_SLOT
TAPS_A = 5
BANK = 512
V_MAIN = BANK // CB
BLOCK = 32
BLOCKS = P // BLOCK
ORDER = (0, 1, 2, 3, 6, 7, 4, 5)
BY_PE = 6
HP, WP = H + 2, W + 2
EPS = 1e-5
QMAX = float(2 ** 15 - 1)
LEAST_MAX = 1e-12
ROUND = 1.5 * 2.0 ** 23
SQRT2 = 1.4142135623730951
LEAST_POWER = 2.0 ** -14

F32 = mybir.dt.float32
BF16 = mybir.dt.bfloat16
I32 = mybir.dt.int32
U8 = mybir.dt.uint8
I8 = mybir.dt.int8
ALU = mybir.AluOpType
ACT = mybir.ActivationFunctionType
AX_X = mybir.AxisListType.X

(V_GN1S, V_GN1B, V_GN2S, V_GN2B, V_GN3S, V_GN3B, V_PEGB, V_BOFF, V_BNG, V_BNB, V_BNM, V_BNV) = (
    0, 1, 2, 3, 4, 8, 12, 13, 14, 18, 22, 26)
V_COLS = 30
Q_W1, Q_PEG, Q_W2, Q_W3 = 0, CH * CB, CH * CB + TAPS, CH * CB + TAPS + TAPS * CB
Q_COLS = Q_W3 + C
C_FOLD, C_COORD, C_ID, C_AVG8, C_DEV8 = 0, CB, CB + H, CB + H + P, CB + H + 2 * P
C_COLS = C_DEV8 + P

PIECES = ((0, 0, 0, 2), (0, 1, 0, 2), (1, 0, 0, 2), (1, 1, 0, 2))

IDLE = (7, 2, 3, 4, 8, 5, 1, 7, 7, 5, 0, 6, 0, 6, 0, 2, 0, 3)


def build(nc, x, first, pairs, consts, woff, grid, w2, w3, wq, out):
    with ExitStack() as ctx:
        def sb(name, shape, dt=F32):
            return ctx.enter_context(nc.sbuf_tensor(name, shape, dt))

        def ps(name, shape):
            return ctx.enter_context(nc.psum_tensor(name, shape, F32))

        def sem(name):
            return ctx.enter_context(nc.semaphore(name))

        x_sb = sb("x_sb", [P, CH, B2, HALVES, N])
        first_sb = sb("first_sb", [P, CH * CB + V_COLS])
        w1_sb = first_sb[:, 0:CH * CB].rearrange("p (c o) -> p c o", c=CH)
        vec = first_sb[:, CH * CB:CH * CB + V_COLS]
        consts_sb = sb("consts_sb", [P, C_COLS])
        pairs_sb = sb("pairs_sb", [P, 2 * P])
        avg2, dev2 = pairs_sb[:, 0:P], pairs_sb[:, P:2 * P]
        ident = consts_sb[:, C_ID:C_ID + P]
        avg8 = consts_sb[:, C_AVG8:C_AVG8 + P]
        dev8 = consts_sb[:, C_DEV8:C_DEV8 + P]
        fold = consts_sb[:, C_FOLD:C_FOLD + CB]
        coord = consts_sb[:, C_COORD:C_COORD + H]
        woff_sb = sb("woff_sb", [P, TAPS, CB])
        grid_sb = sb("grid_sb", [CB, PIX])
        w2_sb = sb("w2_sb", [P, TAPS * CB])
        w3_sb = sb("w3_sb", [P, HALVES, C])
        wq_sb = sb("wq_sb", [P, Q_COLS])
        wq_mag = sb("wq_mag", [P, Q_COLS])
        wq_sign = sb("wq_sign", [P, Q_COLS])
        wqb = sb("wqb", [P, Q_COLS], BF16)
        pegq = sb("pegq", [P, TAPS, CB], BF16)
        feat = sb("feat", [P, B2, HP, WP])
        feat_flat = sb("feat_flat", [P, PIX])
        om_sb = sb("om_sb", [P, PIX])
        omt_sb = sb("omt_sb", [P, B2, NQ, HALVES, OFF_ROWS])
        mask = sb("mask", [P, B2, NQ, HALVES, TAPS])
        hats = sb("hats", [P, T, HALVES, 2, TAPS, H])
        g_rows = [sb(f"g_rows{i}", [P, TAPS, H, W]) for i in range(3)]
        g_cols = [sb(f"g_cols{h}", [P, TAPS * NQ, NQ, P]) for h in range(HALVES)]
        g_last = [sb(f"g_last{h}", [P, TAPS * NQ, P]) for h in range(HALVES)]
        g_blocks = sb("g_blocks", [P, BLOCKS, HALVES, TAPS * NQ, BLOCK])
        g_placed = sb("g_placed", [P, BLOCKS, HALVES, TAPS * NQ, BLOCK])
        v_sb = sb("v_sb", [P, B, NQ, TAPS, CB])
        feat2 = sb("feat2", [P, B2, N])
        blocks_flat = g_blocks[:].rearrange("p i h k n -> p (i h k n)")
        SIZE = CH * PIX * HALVES

        def pieces(t):
            return t.rearrange("p (c b h n) -> p c b h n", c=CH, b=B2, h=HALVES)

        y0 = pieces(blocks_flat[:, 0:SIZE])
        act = sb("act", [P, B2, N])
        quot, res = (pieces(g_cols[h][:].rearrange("p k q n -> p (k q n)")[:, 0:SIZE]) for h in range(HALVES))
        n1_hi, n1_lo = (pieces(blocks_flat[:, SIZE + SIZE // 2 * i:SIZE + SIZE // 2 * (i + 1)].bitcast(BF16))
                        for i in range(2))
        pads = [sb(f"pad{i}", [P, B2, HALVES, HP, WP], BF16) for i in range(2)]
        n4 = sb("n4", [P, B2, HALVES, N], BF16)
        raw = sb("raw", [P, B2, N])
        zeros = sb("zeros", [P, BANK], BF16)
        tiny_sb = sb("tiny_sb", [P, 1])
        zero_sb = sb("zero_sb", [P, 1])
        eps_sb = sb("eps_sb", [P, 1])
        stats = sb("stats", [P, B2, 4, 6])
        mv = sb("mv", [P, B2, 4, 2])
        var = sb("var", [P, B2, 4])
        dev_sb = sb("dev_sb", [P, B2, 4])
        std = sb("std", [P, B2, 4])
        rstd = sb("rstd", [P, B2, 4])
        gn_scale = sb("gn_scale", [P, B2, 4])
        mean_gamma = sb("mean_gamma", [P, B2, 4])
        gn_bias = sb("gn_bias", [P, B2, 4])
        bn_std = sb("bn_std", [P, 4])
        bn_inv = sb("bn_inv", [P, 4])
        bn_off = sb("bn_off", [P, 4])
        piece_max = sb("piece_max", [P, B2, 4])
        mx = sb("mx", [P, 5, B2])
        unused = sb("unused", [P, P])
        first_max = sb("first_max", [P, 5])
        first_scale = sb("first_scale", [P, 5])
        q_inv = sb("q_inv", [P, 5])
        q_scale = sb("q_scale", [P, 5])
        q_floor = sb("q_floor", [P, 1])
        bn_minus = sb("bn_minus", [P, 2])
        bn_mul = sb("bn_mul", [P, 4])

        slot = [ps(f"slot{i}", [P, 2 * BANK]) for i in range(3)]
        acc = [ps(f"acc{b2}", [P, BANK]) for b2 in range(B2)]
        small = [slot[2][:, BANK * b2:BANK * b2 + BANK] for b2 in range(B2)]

        first_in, pairs_in, consts_in, woff_in, grid_in, w2_in, w3_in, wq_in, stored = (
            sem(n) for n in ("first_in", "pairs_in", "consts_in", "woff_in", "grid_in", "w2_in", "w3_in", "wq_in",
                             "stored"))
        x_in = [[sem(f"x_in{b2}{c}") for c in range(CH)] for b2 in range(B2)]
        zeros_ready = sem("zeros_ready")
        pads_zero = sem("pads_zero")
        bn_var_ready = sem("bn_var_ready")
        bn_std_ready = sem("bn_std_ready")
        conv1_done = sem("conv1_done")
        mv_ready = sem("mv_ready")
        sums_done = sem("sums_done")
        sq_ready = sem("sq_ready")
        sq_done = sem("sq_done")
        var_ready = sem("var_ready")
        std_ready = sem("std_ready")
        gn_ready = sem("gn_ready")
        feat_ready = sem("feat_ready")
        flat_ready = sem("flat_ready")
        om_done = sem("om_done")
        om_ready = sem("om_ready")
        om_rest_ready = sem("om_rest_ready")
        omt_done = sem("omt_done")
        omt_ready = sem("omt_ready")
        mask_ready = sem("mask_ready")
        diff_ready = sem("diff_ready")
        abs_ready = sem("abs_ready")
        hats_made = sem("hats_made")
        hats_cut = sem("hats_cut")
        hats_ready = sem("hats_ready")
        v_done = sem("v_done")
        v_ready = sem("v_ready")
        g_ready = sem("g_ready")
        turned = sem("turned")
        g_copied = sem("g_copied")
        blocks_turned = sem("blocks_turned")
        blocks_placed = [sem(f"blocks_placed{i}") for i in range(2)]
        sampled = sem("sampled")
        feat2_ready = sem("feat2_ready")
        conv3_done = sem("conv3_done")
        norm3_ready = sem("norm3_ready")
        half_read = sem("half_read")
        sign_ready = sem("sign_ready")
        wq_ready = sem("wq_ready")
        placed = sem("placed")
        max_ready = sem("max_ready")
        max_spread = sem("max_spread")
        relu_ready = sem("relu_ready")
        quot_ready = sem("quot_ready")
        lo_ready = sem("lo_ready")
        hi_ready = sem("hi_ready")
        qconv_done = sem("qconv_done")
        raw_ready = sem("raw_ready")
        act_ready = sem("act_ready")
        sum_ready = sem("sum_ready")
        half_ready = sem("half_ready")
        res_ready = sem("res_ready")
        chain = sem("dve_chain")

        block = ctx.enter_context(nc.Block())

        def window(tile, b2, k):
            dy, dx = k // 3, k % 3
            return tile[:, b2, dy:dy + H, dx:dx + W]

        def inner(tile, b2):
            return tile[:, b2, 1:1 + H, 1:1 + W]

        def image(t):
            return t.rearrange("p (y x) -> p y x", y=H)

        def rows(h):
            return slice(CB * h, CB * h + CB)

        def flat(t):
            return t.rearrange("p h n -> p (h n)")

        x_v = x.rearrange("(h b) (c p) n -> b c p h n", h=HALVES, c=CH)
        out_v = out.rearrange("(h b) (c p) n -> b c p h n", h=HALVES, c=CH)

        def blocks_in_place(engine):
            engine.wait_ge(blocks_placed[0], 16 * BLOCKS * (BLOCKS - 1))
            engine.wait_ge(blocks_placed[1], 16 * BLOCKS)

        def place_blocks(queue, groups, placed):
            for j in range(BLOCKS):
                queue.wait_ge(blocks_turned, HALVES * (j + 1))
                for i in groups:
                    queue.dma_start(g_placed[BLOCK * j:BLOCK * j + BLOCK, i].rearrange("p h k n -> p (h k n)"),
                                    g_blocks[BLOCK * i:BLOCK * i + BLOCK, j].rearrange("p h k n -> p (h k n)")
                                    ).then_inc(placed, 16)

        @block.sync
        def _(sp):
            sp.dma_start(first_sb[:], first).then_inc(first_in, 16)
            sp.dma_start(x_sb[:, 1, 0], x_v[0, 1]).then_inc(x_in[0][1], 16)
            sp.dma_start(pairs_sb[:], pairs).then_inc(pairs_in, 16)
            for c in range(CH):
                sp.dma_start(x_sb[:, c, 1], x_v[1, c]).then_inc(x_in[1][c], 16)
            sp.dma_start(woff_sb[:], woff).then_inc(woff_in, 16)
            sp.dma_start(grid_sb[:], grid).then_inc(grid_in, 16)
            sp.dma_start(consts_sb[:], consts).then_inc(consts_in, 16)
            sp.dma_start(w2_sb[:], w2).then_inc(w2_in, 16)
            sp.dma_start(wq_sb[:], wq).then_inc(wq_in, 16)
            sp.dma_start(w3_sb[:], w3).then_inc(w3_in, 16)
            place_blocks(sp, range(BLOCKS - 1), blocks_placed[0])
            for i, (c, b2, h, n) in enumerate(PIECES):
                sp.wait_ge(res_ready, i + 1)
                if i == len(PIECES) - 1:
                    sp.wait_ge(half_ready, 1)
                sp.dma_start(out_v[b2, c, :, h:h + n], res[:, c, b2, h:h + n]).then_inc(stored, 16)
            sp.wait_ge(stored, 16 * len(PIECES))

        @block.gpsimd
        def _(pool):
            nc.gpsimd.memset(feat[:], 0.0).then_inc(pads_zero, 1)
            for t in pads:
                nc.gpsimd.memset(t[:], 0.0).then_inc(pads_zero, 1)
            for b2 in range(B2):
                pool.wait_ge(feat_ready, b2 + 1)
                nc.gpsimd.tensor_copy(image(feat_flat[:, N * b2:N * b2 + N]), inner(feat, b2)).then_inc(flat_ready, 1)
            for t in range(T):
                if t == 0:
                    pool.wait_ge(hats_made, 1)
                else:
                    pool.wait_ge(abs_ready, t)
                    v = hats[:, t].rearrange("p h a k y -> p (h a k y)")
                    nc.gpsimd.tensor_scalar(v, v, 1.0, 1.0, ALU.min, ALU.subtract).then_inc(hats_cut, 1)
                    pool.wait_ge(hats_cut, t)
                pool.wait_ge(mask_ready, t // NQ + 1)
                nc.gpsimd.tensor_tensor(hats[:, t, :, 1], hats[:, t, :, 1],
                                        mask[:, t // NQ, t % NQ].unsqueeze(3).to_broadcast([P, HALVES, TAPS, H]),
                                        ALU.mult).then_inc(hats_ready, 1)
            place_blocks(pool, range(BLOCKS - 1, BLOCKS), blocks_placed[1])
            pool.wait_ge(wq_ready, 1)
            nc.gpsimd.tensor_tensor(
                pegq[:], fold.unsqueeze(1).to_broadcast([P, TAPS, CB]),
                wqb[:, Q_PEG:Q_PEG + TAPS].unsqueeze(2).to_broadcast([P, TAPS, CB]), ALU.mult).then_inc(placed, 1)

        @block.tensor
        def _(pe):
            def idle(n, bank):
                for _ in range(n):
                    nc.tensor.matmul(bank, zeros[:, 0:P], zeros[:], start=True, stop=True)

            spare = slot[1][:, BANK:2 * BANK]

            pe.wait_ge(zeros_ready, 1)
            idle(IDLE[0], spare)
            def conv1(b2):
                for c in range(CH):
                    pe.wait_ge(x_in[b2][c], 16)
                    for h in range(HALVES):
                        mm = nc.tensor.matmul(acc[b2][rows(h), 0:N], w1_sb[:, c, :], x_sb[:, c, b2, h, :],
                                              start=(c == 0), stop=(c == CH - 1))
                mm.then_inc(conv1_done, 1)

            def pair_sums(n, b2):
                pe.wait_ge(mv_ready, n)
                nc.tensor.matmul(small[b2][:, 0:2], avg2, mv[:, b2, 0, :], start=True, stop=True)
                nc.tensor.matmul(small[b2][:, 4:5], dev2, mv[:, b2, 0, 0:1], start=True, stop=True
                                 ).then_inc(sums_done, 1)

            pe.wait_ge(first_in, 16)
            conv1(0)
            idle(IDLE[1], spare)
            pe.wait_ge(pairs_in, 16)
            pair_sums(1, 0)
            conv1(1)
            idle(IDLE[2], spare)
            pair_sums(2, 1)

            def om_step(b2, s):
                for p in range(2):
                    k = s + TAPS_A * p
                    if k < TAPS:
                        mm = nc.tensor.matmul(slot[0][CB * p:CB * p + CB, BANK * b2:BANK * b2 + N],
                                              woff_sb[:, k, :], window(feat, b2, k), start=(s == 0),
                                              stop=(k in (TAPS_A - 1, TAPS - 1)))
                return mm

            def om_turn(b2):
                pe.wait_ge(om_ready, b2 + 1)
                pe.wait_ge(om_rest_ready, b2 + 1)
                for q in range(NQ):
                    at = N * b2 + P * q
                    mm = nc.tensor.matmul(slot[1][:, BANK * b2 + CB * q:BANK * b2 + CB * q + CB],
                                          om_sb[:, at:at + P], fold, start=True, stop=True)
                mm.then_inc(omt_done, 1)

            pe.wait_ge(woff_in, 16)
            for b2 in range(B2):
                pe.wait_ge(feat_ready, b2 + 1)
                for s in range(TAPS_A):
                    mm = om_step(b2, s)
                    if b2 == 1 and s == 1:
                        pe.wait_ge(consts_in, 16)
                        om_turn(0)
                mm.then_inc(om_done, 1)

            v_banks = [small[0], small[1], acc[0][:], acc[1][:]]
            pe.wait_ge(w2_in, 16)

            def make_v(i):
                b2, q, h = i // 4, i // 2 % 2, i % 2
                pe.wait_ge(flat_ready, b2 + 1)
                if i >= 4:
                    pe.wait_ge(v_ready, i - 3)
                at = N * b2 + P * q
                lhs = feat_flat[rows(h), at:at + P]
                nc.tensor.matmul(v_banks[i % 4], lhs, w2_sb[rows(h), 0:BANK], start=True, stop=True
                                 ).then_inc(v_done, 1)

            def make_last_v(i):
                b2, q, h = i // 4, i // 2 % 2, i % 2
                at = BANK * h + CB * (i // 2)
                return nc.tensor.matmul(slot[0][:, at:at + CB], feat_flat[rows(h), N * b2 + P * q:N * b2 + P * q + P],
                                        w2_sb[rows(h), BANK:TAPS * CB], start=True, stop=True)

            make_v(0)
            make_v(1)
            om_turn(1)
            make_last_v(0)
            make_last_v(1)
            for i in range(2, 2 * T):
                make_v(i)
                mm = make_last_v(i)
            mm.then_inc(v_done, 1)

            slot_of = (1, 2, 0)

            def turn(i):
                pe.wait_ge(g_ready, i + 1)
                for j in range(TURNS):
                    if i == 0:
                        pe.wait_ge(v_ready, (1, 6, 2 * T + 1)[j])
                    else:
                        pe.wait_ge(g_copied, TURNS * (i - 1) + j + 1)
                    for k in range(PER_SLOT * j, PER_SLOT * j + PER_SLOT):
                        for q in range(NQ):
                            at = P * (NQ * (k - PER_SLOT * j) + q)
                            mm = nc.tensor.transpose(slot[slot_of[j]][:, at:at + P],
                                                     g_rows[i % 3][:, k, ROWS_Q * q:ROWS_Q * q + ROWS_Q, :], ident)
                    mm.then_inc(turned, 1)

            def sample(first_tap, last_tap):
                for k in range(first_tap, last_tap + 1):
                    pe.wait_ge(g_copied, TURNS * 3 + k // PER_SLOT + 1)
                    for q in range(NQ):
                        for h in range(HALVES):
                            mm = nc.tensor.matmul(
                                acc[0][rows(h), 0:N], v_sb[:, B2 * h, q, k, :],
                                g_cols[h][:, NQ * k + q].rearrange("p a n -> p (a n)"),
                                start=(k == 0 and q == 0), stop=(k == TAPS - 1 and q == NQ - 1))
                return mm

            def sample_half(t, first_tap, last_tap):
                for k in range(first_tap, last_tap + 1):
                    if t % NQ == 1:
                        pe.wait_ge(g_copied, TURNS * (BY_PE - 1) + k // PER_SLOT + 1)
                    else:
                        blocks_in_place(pe)
                    for q in range(NQ):
                        for h in range(HALVES):
                            at = P * (t % NQ)
                            mm = nc.tensor.matmul(
                                acc[1][rows(h), at:at + P], v_sb[:, B2 * h + 1, q, k, :],
                                g_last[h][:, NQ * k + q, :] if t % NQ == 1 else g_placed[:, :, h, NQ * k + q, :],
                                start=(k == 0 and q == 0), stop=(k == TAPS - 1 and q == NQ - 1))
                return mm

            for i in range(5):
                turn(i)
            sample(0, 2)
            turn(5)
            sample(3, 8).then_inc(sampled, 1)

            def conv3(b2):
                pe.wait_ge(feat2_ready, b2 + 1)
                for c in range(CH):
                    for h in range(HALVES):
                        mm = nc.tensor.matmul(slot[c][:, BANK * b2 + N * h:BANK * b2 + N * h + N],
                                              w3_sb[:, h, P * c:P * c + P], feat2[:, b2, :],
                                              start=True, stop=True)
                    mm.then_inc(conv3_done, 1)

            def eight_means(b2):
                pe.wait_ge(mv_ready, 4 + 2 * b2)
                nc.tensor.matmul(small[b2][:, 8:12], avg8, mv[:, b2, :, 0], start=True, stop=True)
                nc.tensor.matmul(small[b2][:, 12:16], dev8, mv[:, b2, :, 0], start=True, stop=True
                                 ).then_inc(sums_done, 1)
                nc.tensor.matmul(acc[0][:, 0:4], avg8, mv[:, b2, :, 1], start=True, stop=False,
                                 skip_group_check=True)

            def eight_vars(b2):
                pe.wait_ge(sq_ready, b2 + 1)
                nc.tensor.matmul(acc[0][:, 0:4], avg8, dev_sb[:, b2, :], start=False, stop=True,
                                 skip_group_check=True
                                 ).then_inc(sq_done, 1)

            def spread_max(n, b2):
                biased = n >= 3
                if biased:
                    pe.wait_ge(raw_ready, B2 * (n - 3) + b2 + 1)
                else:
                    pe.wait_ge(max_ready, B2 * (n - 1) + b2 + 1)
                nc.tensor.matmul(small[b2][:, P:2 * P], mx[:, n, b2:b2 + 1].to_broadcast([P, P]), ident,
                                 start=not biased, stop=True, is_transpose=not biased,
                                 skip_group_check=True).then_inc(max_spread, 1)

            def spread_bias(n, b2):
                nc.tensor.matmul(small[b2][:, P:2 * P], bn_off[:, n - 3:n - 2].to_broadcast([P, P]), ident,
                                 start=True, stop=False, skip_group_check=True)

            sample_half(3, 0, 1)
            pe.wait_ge(g_copied, TURNS * (BY_PE - 1) + 2)
            pair_sums(3, 0)
            sample_half(3, 2, 6)
            pe.wait_ge(w3_in, 16)
            conv3(0)
            sample_half(3, 7, 8)
            sample_half(2, 0, 1)
            eight_means(0)
            sample_half(2, 2, 3)
            eight_vars(0)
            sample_half(2, 4, 8).then_inc(sampled, 1)
            idle(IDLE[3], spare)
            pair_sums(5, 1)
            idle(IDLE[4], spare)
            conv3(1)
            spread_max(1, 0)
            idle(IDLE[5], acc[1][:])
            eight_means(1)
            idle(IDLE[6], acc[1][:])
            eight_vars(1)
            idle(IDLE[7], acc[1][:])
            spread_max(1, 1)
            idle(IDLE[8], spare)
            for b2 in range(B2):
                for part, ready in ((n1_lo, lo_ready), (n1_hi, hi_ready)):
                    if part is n1_hi or b2 == 1:
                        idle(IDLE[14 + (part is n1_hi) + 2 * b2 - 1], spare)
                    for c in range(CH):
                        pe.wait_ge(ready, CH * b2 + c + 1)
                        for h in range(HALVES):
                            mm = nc.tensor.matmul(acc[b2][rows(h), 0:N], wqb[:, Q_W1 + CB * c:Q_W1 + CB * c + CB],
                                                  part[:, c, b2, h, :], start=(part is n1_lo and c == 0),
                                                  stop=(part is n1_hi and c == CH - 1))
                mm.then_inc(qconv_done, 1)
                if b2 == 1:
                    spread_max(2, 0)
                    idle(IDLE[17], spare)
                    spread_max(2, 1)
            idle(IDLE[9], spare)

            def parts_ready(n, b2):
                pe.wait_ge(lo_ready, CH * B2 + HALVES * (B2 * (n - 2) + b2 + 1))
                pe.wait_ge(hi_ready, CH * B2 + HALVES * (B2 * (n - 2) + b2 + 1))

            def window_conv(weights, pad, n):
                for b2 in range(B2):
                    parts_ready(n, b2)
                    for k in range(TAPS):
                        for h in range(HALVES):
                            mm = nc.tensor.matmul(acc[b2][rows(h), 0:N], weights(k), window(pad[:, b2], h, k),
                                                  start=(k == 0), stop=(k == TAPS - 1))
                    mm.then_inc(qconv_done, 1)
                for b2 in range(B2):
                    spread_bias(n + 1, b2)
                spread_max(n + 1, 0)
                idle(IDLE[10 + 2 * (n - 2)], spare)
                spread_max(n + 1, 1)
                idle(IDLE[11 + 2 * (n - 2)], spare)

            pe.wait_ge(placed, 1)
            window_conv(lambda k: pegq[:, k, :], pads[0], 2)
            window_conv(lambda k: wqb[:, Q_W2 + CB * k:Q_W2 + CB * k + CB], pads[1], 3)
            for c in range(CH):
                for b2 in range(B2):
                    parts_ready(4, b2)
                    nc.tensor.matmul(slot[c][:, BANK * b2:BANK * b2 + BANK], wqb[:, Q_W3 + P * c:Q_W3 + P * c + P],
                                     flat(n4[:, b2]), start=True, stop=True).then_inc(qconv_done, 1)

        @block.scalar
        def _(a):
            a.dma_start(x_sb[:, 0, 0], x_v[0, 0]).then_inc(x_in[0][0], 16)
            nc.scalar.preload_act_table(ACT.Sqrt)
            a.wait_ge(bn_var_ready, 1)
            nc.scalar.activation(bn_std[:], bn_std[:], ACT.Sqrt).then_inc(bn_std_ready, 1)

            def root(done, b2):
                a.wait_ge(var_ready, done)
                nc.scalar.activation(std[:, b2, 0:1], var[:, b2, 0:1], ACT.Sqrt, bias=eps_sb[:, 0:1]
                                     ).then_inc(std_ready, 1)

            def normalise(done, b2, dst, src, ready):
                a.wait_ge(gn_ready, 2 * done)
                nc.scalar.activation(dst, src, ACT.Relu, bias=gn_bias[:, b2, 0:1], scale=gn_scale[:, b2, 0:1]
                                     ).then_inc(ready, 1)

            root(1, 0)
            a.wait_ge(pads_zero, 1)
            normalise(1, 0, inner(feat, 0), image(acc[0][:, 0:N]), feat_ready)
            root(2, 1)
            normalise(2, 1, inner(feat, 1), image(acc[1][:, 0:N]), feat_ready)
            def copy_om_rest(b2):
                a.wait_ge(om_done, b2 + 1)
                nc.scalar.activation(om_sb[CB:P, N * b2:N * b2 + N], slot[0][CB:P, BANK * b2:BANK * b2 + N],
                                     ACT.Copy).then_inc(om_rest_ready, 1)

            def make_mask(b2):
                a.wait_ge(omt_ready, b2 + 1)
                nc.scalar.activation(mask[:, b2], omt_sb[:, b2, :, :, 2 * TAPS:OFF], ACT.Sigmoid
                                     ).then_inc(mask_ready, 1)

            def copy_omt(b2):
                a.wait_ge(omt_done, b2 + 1)
                nc.scalar.activation(omt_sb[:, b2].rearrange("p q h o -> p (q h o)"),
                                     slot[1][:, BANK * b2:BANK * b2 + NQ * CB], ACT.Copy).then_inc(omt_ready, 1)
                make_mask(b2)

            def distance(t):
                a.wait_ge(diff_ready, t)
                v = hats[:, t].rearrange("p h a k y -> p (h a k y)")
                nc.scalar.activation(v, v, ACT.Abs).then_inc(abs_ready, 1)

            v_banks = [small[0], small[1], acc[0][:], acc[1][:]]

            def copy_v(i):
                b2, q, h = i // 4, i // 2 % 2, i % 2
                a.wait_ge(v_done, i + 1)
                nc.scalar.activation(v_sb[:, B2 * h + b2, q, 0:V_MAIN, :].rearrange("p k o -> p (k o)"),
                                     v_banks[i % 4], ACT.Copy).then_inc(v_ready, 1)

            copy_om_rest(0)
            nc.scalar.preload_act_table(ACT.Sigmoid)
            make_mask(0)
            copy_om_rest(1)
            copy_v(0)
            distance(1)
            copy_v(1)
            copy_omt(1)
            for i in range(2, 2 * T):
                copy_v(i)
                if i in (4, 5):
                    distance(i - 2)
            a.wait_ge(v_done, 2 * T + 1)
            for h in range(HALVES):
                last = nc.scalar.activation(v_sb[:, B2 * h:B2 * h + B2, :, V_MAIN, :],
                                            slot[0][:, BANK * h:BANK * h + T * CB].rearrange(
                                                "p (b q o) -> p b q o", b=B2, q=NQ), ACT.Copy)
            last.then_inc(v_ready, 1)

            def copy_g(i):
                t, h = ORDER[i] // HALVES, ORDER[i] % HALVES
                for j in range(TURNS):
                    a.wait_ge(turned, TURNS * i + j + 1)
                    per = PER_SLOT * NQ
                    dst = g_cols[h][:, :, t, :] if t < NQ else g_last[h][:]
                    nc.scalar.activation(dst[:, per * j:per * j + per, :],
                                         slot[(1, 2, 0)[j]][:, 0:per * P].rearrange("p (k n) -> p k n", k=per),
                                         ACT.Copy).then_inc(g_copied, 1)

            for i in range(BY_PE):
                copy_g(i)
                if i == 4:
                    a.wait_ge(wq_in, 16)
                    nc.scalar.activation(wq_sign[:], wq_sb[:], ACT.Sign).then_inc(sign_ready, 1)
                    nc.scalar.activation(wq_mag[:], wq_sb[:], ACT.Abs).then_inc(sign_ready, 1)
            a.wait_ge(sign_ready, 2)
            nc.scalar.activation(wq_mag[:], wq_mag[:], ACT.Identity, scale=SQRT2, bias=tiny_sb[:, 0:1]
                                 ).then_inc(sign_ready, 1)
            nc.scalar.preload_act_table(ACT.Sqrt)

            def norm3(b2):
                a.wait_ge(gn_ready, 2 * (4 + 2 * b2))
                blocks_in_place(a)
                for i in (0, 1, 2):
                    c, h = i // HALVES, i % HALVES
                    if c == 1:
                        a.wait_ge(half_read, b2 + 1)
                    nc.scalar.activation(y0[:, c, b2, h, :], slot[c][:, BANK * b2 + N * h:BANK * b2 + N * h + N],
                                         ACT.Identity, bias=gn_bias[:, b2, i:i + 1], scale=gn_scale[:, b2, i:i + 1]
                                         ).then_inc(norm3_ready, 1)

            def relu0(b2):
                a.wait_ge(sum_ready, 4 * b2 + 4)
                nc.scalar.activation(flat(y0[:, 0, b2]), flat(y0[:, 0, b2]), ACT.Relu).then_inc(relu_ready, 1)

            def root4(b2):
                a.wait_ge(sums_done, 4 + 2 * b2)
                nc.scalar.activation(dev_sb[:, b2, :], small[b2][:, 12:16], ACT.Square).then_inc(sq_ready, 1)
                a.wait_ge(sq_done, b2 + 1)
                nc.scalar.activation(std[:, b2, :], acc[0][:, 0:4], ACT.Sqrt, bias=eps_sb[:, 0:1]
                                     ).then_inc(std_ready, 1)

            root(3, 0)
            normalise(3, 0, feat2[:, 0, :], acc[0][:, 0:N], feat2_ready)
            root4(0)
            norm3(0)
            root(4, 1)
            normalise(5, 1, feat2[:, 1, :], acc[1][:, 0:N], feat2_ready)
            relu0(0)
            root4(1)
            norm3(1)
            relu0(1)

            def high_part(dst, src, done):
                a.wait_ge(quot_ready, done)
                nc.scalar.activation(dst, src, ACT.Copy, scale=256.0).then_inc(hi_ready, 1)

            def byte(t, n, dt):
                return t.bitcast(dt).rearrange("p (n e) -> p n e", e=4)[:, :, n]

            for b2 in range(B2):
                for c in range(CH):
                    high_part(flat(n1_hi[:, c, b2]), byte(flat(quot[:, c, b2]), 1, I8), CH * b2 + c + 1)
            q2 = quot[:, 0, 0].rearrange("p b n -> p (b n)")

            def high_parts(n, dst):
                for b2 in range(B2):
                    for h in range(HALVES):
                        src = byte(q2[rows(h), N * b2:N * b2 + N], 1, I8)
                        high_part(dst(b2, h), image(src) if n < 4 else src, CH * B2 + B2 * (n - 2) + b2 + 1)

            a.wait_ge(pads_zero, 3)
            for n in (2, 3):
                high_parts(n, lambda b2, h: inner(pads[n - 2][CB:P, b2], h))
                for b2 in range(B2):
                    a.wait_ge(raw_ready, B2 * (n - 2) + b2 + 1)
                    nc.scalar.activation(act[:, b2, :], raw[:, b2, :], ACT.Relu, bias=bn_off[:, n - 2:n - 1]
                                         ).then_inc(act_ready, 1)
            high_parts(4, lambda b2, h: n4[CB:P, b2, h, :])
            for i, (c, b2, h, n) in enumerate(PIECES):
                a.wait_ge(sum_ready, 4 * B2 + i + 1)
                if i == len(PIECES) - 1:
                    n = 1
                piece = flat(res[:, c, b2, h:h + n])
                nc.scalar.activation(piece, piece, ACT.Relu, bias=bn_off[:, 2 + c:3 + c]).then_inc(res_ready, 1)

        @block.vector
        def _(dve):
            count = [0]

            def settle(ins):
                count[0] += 1
                ins.then_inc(chain, 1)
                dve.wait_ge(chain, count[0])

            def before_next(ins):
                count[0] += 1
                ins.then_inc(chain, 1)

            tt, ts, stt = nc.vector.tensor_tensor, nc.vector.tensor_scalar, nc.vector.scalar_tensor_tensor
            nc.vector.memset(zeros[:], 0.0).then_inc(zeros_ready, 1)
            nc.vector.memset(eps_sb[:], EPS)
            nc.vector.memset(zero_sb[:], 0.0)
            nc.vector.memset(tiny_sb[:], 1e-20 * SQRT2)
            dve.wait_ge(first_in, 16)
            ts(bn_std[:], vec[:, V_BNV:V_BNV + 4], EPS, None, ALU.add).then_inc(bn_var_ready, 1)
            def moments(b2):
                settle(nc.vector.bn_stats(stats[:, b2, 0, :], acc[b2][:, 0:N]))
                nc.vector.bn_aggr(mv[:, b2, 0, :], stats[:, b2, 0, :]).then_inc(mv_ready, 1)

            def pair_var(done, b2):
                dve.wait_ge(sums_done, done)
                ts(var[:, b2, 0:1], small[b2][:, 4:5], small[b2][:, 4:5], small[b2][:, 1:2], ALU.mult, ALU.add
                   ).then_inc(var_ready, 1)

            def pair_scale(done, b2, gamma, beta):
                before_next(tt(mean_gamma[:, b2, 0:1], small[b2][:, 0:1], vec[:, gamma:gamma + 1], ALU.mult))
                dve.wait_ge(std_ready, done)
                settle(nc.vector.reciprocal(rstd[:, b2, 0:1], std[:, b2, 0:1]))
                tt(gn_scale[:, b2, 0:1], rstd[:, b2, 0:1], vec[:, gamma:gamma + 1], ALU.mult).then_inc(gn_ready, 1)
                stt(gn_bias[:, b2, 0:1], mean_gamma[:, b2, 0:1], rstd[:, b2, 0:1], vec[:, beta:beta + 1], ALU.mult,
                    ALU.subtract, reverse1=True).then_inc(gn_ready, 1)

            dve.wait_ge(conv1_done, 1)
            moments(0)
            pair_var(1, 0)
            pair_scale(1, 0, V_GN1S, V_GN1B)
            dve.wait_ge(conv1_done, 2)
            moments(1)
            pair_var(2, 1)
            pair_scale(2, 1, V_GN1S, V_GN1B)

            def add_grid(b2):
                dve.wait_ge(om_done, b2 + 1)
                stt(om_sb[0:CB, N * b2:N * b2 + N], slot[0][0:CB, BANK * b2:BANK * b2 + N],
                    vec[0:CB, V_BOFF:V_BOFF + 1], grid_sb[:, N * b2:N * b2 + N], ALU.add, ALU.add
                    ).then_inc(om_ready, 1)

            def differences(t):
                dve.wait_ge(omt_ready, t // NQ + 1)
                return tt(hats[:, t].rearrange("p h a k y -> p h (a k) y"),
                          omt_sb[:, t // NQ, t % NQ, :, 0:2 * TAPS].unsqueeze(3).to_broadcast(
                              [P, HALVES, 2 * TAPS, H]),
                          coord.unsqueeze(1).unsqueeze(1).to_broadcast([P, HALVES, 2 * TAPS, H]), ALU.subtract)

            def make_hats(t):
                v = hats[:, t].rearrange("p h a k y -> p (h a k y)")
                settle(ts(v.bitcast(I32), v.bitcast(I32), 0x7FFFFFFF, None, ALU.bitwise_and))
                ts(v, v, 1.0, 1.0, ALU.min, ALU.subtract).then_inc(hats_made, 1)

            def make_g(i):
                t, h = ORDER[i] // HALVES, ORDER[i] % HALVES
                dve.wait_ge(hats_ready, t + 1)
                if i >= 3:
                    dve.wait_ge(turned, TURNS * (i - 2))
                tt(g_rows[i % 3][:], hats[:, t, h, 1].unsqueeze(3).to_broadcast([P, TAPS, H, W]),
                   hats[:, t, h, 0].unsqueeze(2).to_broadcast([P, TAPS, H, W]), ALU.mult).then_inc(g_ready, 1)

            dve.wait_ge(grid_in, 16)
            dve.wait_ge(consts_in, 16)
            add_grid(0)
            dve.wait_ge(bn_std_ready, 1)
            settle(nc.vector.reciprocal(bn_std[:], bn_std[:]))
            settle(tt(bn_inv[:], bn_std[:], vec[:, V_BNG:V_BNG + 4], ALU.mult))
            settle(tt(bn_off[:], bn_inv[:], vec[:, V_BNM:V_BNM + 4], ALU.mult))
            settle(tt(bn_off[:], vec[:, V_BNB:V_BNB + 4], bn_off[:], ALU.subtract))
            settle(stt(bn_off[:, 0:1], bn_inv[:, 0:1], vec[:, V_PEGB:V_PEGB + 1], bn_off[:, 0:1], ALU.mult, ALU.add))
            settle(ts(bn_minus[:], bn_off[:, 0:2], -1.0, None, ALU.mult))

            dve.wait_ge(omt_done, 1)
            nc.vector.tensor_copy(omt_sb[:, 0].rearrange("p q h o -> p (q h o)"), slot[1][:, 0:NQ * CB]
                                  ).then_inc(omt_ready, 1)
            last = differences(0)
            add_grid(1)
            settle(last)
            make_hats(0)
            differences(1).then_inc(diff_ready, 1)
            make_g(0)
            for t in (2, 3):
                differences(t).then_inc(diff_ready, 1)
            for i in range(1, 2 * T):
                make_g(i)
            dve.wait_ge(g_ready, 2 * T)
            for j in range(BLOCKS):
                for h in range(HALVES):
                    g = g_rows[(BY_PE + h) % 3][:].rearrange("p k y x -> p (k y x)").rearrange(
                        "p (k j r) -> p k j r", j=BLOCKS, r=BLOCK)
                    nc.vector.transpose(g_blocks[:, j, h], g[:, :, j, :]).then_inc(blocks_turned, 1)

            def eight_moments(b2):
                for c in range(CH):
                    dve.wait_ge(conv3_done, CH * b2 + c + 1)
                    for h in range(HALVES):
                        last = nc.vector.bn_stats(stats[:, b2, HALVES * c + h, :],
                                                  slot[c][:, BANK * b2 + N * h:BANK * b2 + N * h + N])
                    settle(last)
                    for i in range(HALVES * c, HALVES * c + HALVES):
                        last = nc.vector.bn_aggr(mv[:, b2, i, :], stats[:, b2, i, :])
                last.then_inc(mv_ready, 1)

            def eight_scale(b2):
                dve.wait_ge(sq_ready, b2 + 1)
                before_next(tt(mean_gamma[:, b2, :], small[b2][:, 8:12], vec[:, V_GN3S:V_GN3S + CH * HALVES],
                               ALU.mult))
                dve.wait_ge(std_ready, 4 + 2 * b2)
                settle(nc.vector.reciprocal(rstd[:, b2, :], std[:, b2, :]))
                tt(gn_scale[:, b2, :], rstd[:, b2, :], vec[:, V_GN3S:V_GN3S + CH * HALVES], ALU.mult
                   ).then_inc(gn_ready, 1)
                settle(tt(dev_sb[:, b2, :], rstd[:, b2, :], mean_gamma[:, b2, :], ALU.mult))
                tt(gn_bias[:, b2, :], vec[:, V_GN3B:V_GN3B + CH * HALVES], dev_sb[:, b2, :], ALU.subtract
                   ).then_inc(gn_ready, 1)

            def norm3(b2):
                dve.wait_ge(gn_ready, 2 * (4 + 2 * b2))
                blocks_in_place(dve)
                ts(y0[:, 1, b2, 1, :], slot[1][:, BANK * b2 + N:BANK * b2 + 2 * N], gn_scale[:, b2, 3:4],
                   gn_bias[:, b2, 3:4], ALU.mult, ALU.add).then_inc(half_read, 1)

            def residual(b2):
                for i, normed in ((3, 0), (0, 1), (1, 2), (2, 3)):
                    c, h = i // HALVES, i % HALVES
                    if normed:
                        dve.wait_ge(norm3_ready, 3 * b2 + normed)
                    else:
                        dve.wait_ge(half_read, b2 + 1)
                    last = nc.vector.tensor_tensor_reduce(y0[:, c, b2, h, :], y0[:, c, b2, h, :], x_sb[:, c, b2, h, :],
                                                          1.0, 0.0, ALU.add, ALU.max, piece_max[:, b2, i:i + 1])
                    last.then_inc(sum_ready, 1)
                dve.wait_ge(sum_ready, 4 * b2 + 4)
                nc.vector.tensor_reduce(mx[:, 1, b2:b2 + 1], piece_max[:, b2, :], AX_X, ALU.max
                                        ).then_inc(max_ready, 1)
                return ts(flat(y0[:, 1, b2]), flat(y0[:, 1, b2]), 0.0, None, ALU.max)

            def first_half_max(n, floor):
                dve.wait_ge(max_spread, B2 * (n - 1) + 1)
                settle(nc.vector.tensor_reduce(first_max[:, n:n + 1], small[0][:, P:2 * P], AX_X, ALU.max))
                settle(ts(first_scale[:, n:n + 1], first_max[:, n:n + 1], floor, 1.0 / QMAX, ALU.max, ALU.mult))

            def make_scale(n):
                dve.wait_ge(max_spread, B2 * (n - 1) + 2)
                settle(nc.vector.tensor_tensor_reduce(unused[:], small[1][:, P:2 * P],
                                                      zero_sb[:].to_broadcast([P, P]), 1.0 / QMAX,
                                                      first_scale[:, n:n + 1], ALU.add, ALU.max,
                                                      q_scale[:, n:n + 1]))
                settle(nc.vector.reciprocal(q_inv[:, n:n + 1], q_scale[:, n:n + 1]))

            dve.wait_ge(sampled, 1)
            moments(0)
            pair_var(3, 0)
            pair_scale(3, 0, V_GN2S, V_GN2B)

            dve.wait_ge(sign_ready, 3)
            settle(ts(wq_mag[:].bitcast(I32), wq_mag[:].bitcast(I32), 0x7F800000, None, ALU.bitwise_and))
            settle(ts(wq_mag[:], wq_mag[:], LEAST_POWER, 1.0, ALU.max, ALU.min))
            tt(wqb[:], wq_mag[:], wq_sign[:], ALU.mult).then_inc(wq_ready, 1)

            eight_moments(0)
            eight_scale(0)
            norm3(0)
            dve.wait_ge(sampled, 2)
            moments(1)
            pair_var(5, 1)
            pair_scale(5, 1, V_GN2S, V_GN2B)
            residual(0)
            eight_moments(1)
            first_half_max(1, LEAST_MAX)
            eight_scale(1)
            norm3(1)
            last = residual(1)
            settle(last)
            make_scale(1)

            def quotient(n, dst, src):
                ts(dst, src, q_inv[:, n:n + 1], ROUND, ALU.mult, ALU.add).then_inc(quot_ready, 1)

            def byte(t, n, dt):
                return t.bitcast(dt).rearrange("p (n e) -> p n e", e=4)[:, :, n]

            def low_part(dst, src, done):
                dve.wait_ge(quot_ready, done)
                nc.vector.tensor_copy(dst, src).then_inc(lo_ready, 1)

            def low1(i):
                b2, c = i // CH, i % CH
                low_part(flat(n1_lo[:, c, b2]), byte(flat(quot[:, c, b2]), 0, U8), i + 1)

            for i in range(B2 * CH):
                b2, c = i // CH, i % CH
                if c == 0:
                    dve.wait_ge(relu_ready, b2 + 1)
                quotient(1, flat(quot[:, c, b2]), flat(y0[:, c, b2]))
                if i > 0:
                    low1(i - 1)
            low1(B2 * CH - 1)

            q2 = quot[:, 0, 0].rearrange("p b n -> p (b n)")

            def parts(n, srcs, dst):
                done = CH * B2 + HALVES * B2 * (n - 2)
                dve.wait_ge(hi_ready, done)
                dve.wait_ge(lo_ready, done)

                def quotients(b2):
                    if n > 2:
                        dve.wait_ge(act_ready, B2 * (n - 3) + b2 + 1)
                    quotient(n, q2[:, N * b2:N * b2 + N], srcs[b2])

                def low_parts(b2):
                    for h in range(HALVES):
                        low = byte(q2[rows(h), N * b2:N * b2 + N], 0, U8)
                        low_part(dst(b2, h), image(low) if n < 4 else low, CH * B2 + B2 * (n - 2) + b2 + 1)

                quotients(0)
                if n == 4:
                    quotients(1)
                    low_parts(0)
                    before_next(ts(bn_mul[:, 2:4], bn_inv[:, 2:4], q_scale[:, 4:5], None, ALU.mult))
                else:
                    low_parts(0)
                    quotients(1)
                low_parts(1)

            for b2 in range(B2):
                dve.wait_ge(qconv_done, b2 + 1)
                nc.vector.tensor_reduce(mx[:, 2, b2:b2 + 1], acc[b2][:, 0:N], AX_X, ALU.max,
                                        apply_absolute_value=True).then_inc(max_ready, 1)
                if b2 == 0:
                    settle(ts(q_floor[:], q_inv[:, 1:2], LEAST_MAX, None, ALU.mult))
            first_half_max(2, q_floor[:, 0:1])
            make_scale(2)
            parts(2, [acc[b2][:, 0:N] for b2 in range(B2)], lambda b2, h: inner(pads[0][0:CB, b2], h))
            settle(tt(q_scale[:, 2:3], q_scale[:, 2:3], q_scale[:, 1:2], ALU.mult))
            settle(tt(bn_mul[:, 0:1], q_scale[:, 2:3], bn_inv[:, 0:1], ALU.mult))
            for n in (3, 4):
                for b2 in range(B2):
                    dve.wait_ge(qconv_done, B2 * (n - 2) + b2 + 1)
                    if n == 4:
                        dve.wait_ge(act_ready, b2 + 1)
                    top = mx[:, n, b2:b2 + 1]
                    nc.vector.tensor_tensor_reduce(raw[:, b2, :], acc[b2][:, 0:N],
                                                   bn_mul[:, n - 3:n - 2].to_broadcast([P, N]), 1.0,
                                                   bn_minus[:, n - 3:n - 2], ALU.mult, ALU.max, top
                                                   ).then_inc(raw_ready, 1)
                first_half_max(n, LEAST_MAX)
                make_scale(n)
                parts(n, [act[:, b2, :] for b2 in range(B2)],
                      (lambda b2, h: inner(pads[1][0:CB, b2], h)) if n == 3 else (lambda b2, h: n4[0:CB, b2, h, :]))
                if n == 3:
                    settle(tt(bn_mul[:, 1:2], q_scale[:, 3:4], bn_inv[:, 1:2], ALU.mult))
            dve.wait_ge(chain, count[0])
            for i, (c, b2, h, n) in enumerate(PIECES):
                dve.wait_ge(qconv_done, 3 * B2 + B2 * c + b2 + 1)
                at = BANK * b2 + N * h
                stt(flat(res[:, c, b2, h:h + n]), slot[c][:, at:at + N * n], bn_mul[:, 2 + c:3 + c],
                    flat(y0[:, c, b2, h:h + n]), ALU.mult, ALU.add).then_inc(sum_ready, 1)
            dve.wait_ge(sum_ready, 4 * B2 + len(PIECES))
            ts(res[:, c, b2, 1, :], res[:, c, b2, 1, :], bn_off[:, 2 + c:3 + c], 0.0, ALU.add, ALU.max
               ).then_inc(half_ready, 1)


def kernel(**inputs):
    import numpy as np
    import concourse.bacc as bacc
    from concourse.bass_utils import run_bass_kernel_spmd as run

    f = np.float32
    a = {k: np.asarray(v) for k, v in inputs.items()}

    first = np.zeros((P, CH * CB + V_COLS), f)
    first[:, 0:CH * CB] = a["L0_conv_w1"][:, :, 0, 0].reshape(CB, CH, P).transpose(2, 1, 0).reshape(P, CH * CB)
    vec = first[:, CH * CB:]

    def both(col, v):
        vec[:CB, col] = v
        vec[CB:, col] = v

    for col, name in ((V_GN1S, "L0_conv_gn1_scale"), (V_GN1B, "L0_conv_gn1_bias"), (V_GN2S, "L0_conv_gn2_scale"),
                      (V_GN2B, "L0_conv_gn2_bias"), (V_PEGB, "L1_conv_peg_b")):
        both(col, a[name])
    for col, name in ((V_GN3S, "L0_conv_gn3_scale"), (V_GN3B, "L0_conv_gn3_bias")):
        vec[:, col:col + CH * HALVES] = np.repeat(a[name].reshape(CH, P).T, HALVES, axis=1)
    for h in range(HALVES):
        vec[OFF_ROWS * h:OFF_ROWS * h + OFF, V_BOFF] = a["L0_conv_b_off"]
    for col, p in ((V_BNG, "g"), (V_BNB, "b"), (V_BNM, "m"), (V_BNV, "v")):
        both(col, a["L1_conv_bn1_" + p])
        both(col + 1, a["L1_conv_bn2_" + p])
        vec[:, col + 2:col + 4] = a["L1_conv_bn3_" + p].reshape(CH, P).T

    consts = np.zeros((P, C_COLS), f)
    eye = np.eye(P, dtype=f)
    consts[:, C_ID:C_ID + P] = eye
    pairs = np.zeros((P, 2 * P), f)
    for g, t, at_avg, at_dev in ((2, pairs, 0, P), (8, consts, C_AVG8, C_DEV8)):
        mean = np.kron(np.eye(P // g, dtype=f), np.full((g, g), 1.0 / g, f))
        t[:, at_avg:at_avg + P] = mean
        t[:, at_dev:at_dev + P] = eye - mean
    for p in range(2):
        consts[CB * p:CB * p + CB, C_FOLD:C_FOLD + CB] = eye[0:CB, 0:CB]
    consts[:, C_COORD:C_COORD + H] = np.arange(H, dtype=f)

    woff = np.zeros((HALVES, CB, TAPS, HALVES, OFF_ROWS), f)
    for h in range(HALVES):
        woff[h, :, :, h, 0:OFF] = a["L0_conv_w_off"].reshape(OFF, CB, TAPS).transpose(1, 2, 0)
    grid = np.zeros((HALVES, OFF_ROWS, B2, H, W), f)
    for k in range(TAPS):
        grid[:, k] = np.arange(W, dtype=f) + (k % 3 - 1)
        grid[:, TAPS + k] = (np.arange(H, dtype=f) + (k // 3 - 1))[:, None]
    w2 = np.zeros((HALVES, CB, TAPS * CB), f)
    w2[:] = a["L0_conv_w2"].reshape(CB, CB, TAPS).transpose(1, 2, 0).reshape(CB, TAPS * CB)
    w3 = np.zeros((HALVES, CB, HALVES, C), f)
    for h in range(HALVES):
        w3[h, :, h] = a["L0_conv_w3"][:, :, 0, 0].T
    wq = np.zeros((HALVES, CB, Q_COLS), f)
    wq.reshape(P, Q_COLS)[:, Q_W1:Q_W1 + CH * CB] = a["L1_conv_w1"][:, :, 0, 0].reshape(CB, CH, P).transpose(
        2, 1, 0).reshape(P, CH * CB)
    wq[:, :, Q_PEG:Q_PEG + TAPS] = a["L1_conv_peg_w"].reshape(CB, TAPS)
    wq[:, :, Q_W2:Q_W2 + TAPS * CB] = a["L1_conv_w2"].reshape(CB, CB, TAPS).transpose(1, 2, 0).reshape(CB, TAPS * CB)
    wq[:, :, Q_W3:Q_W3 + C] = a["L1_conv_w3"][:, :, 0, 0].T

    arrays = {
        "x": np.ascontiguousarray(a["x"]).reshape(B, C, N), "first": first, "pairs": pairs, "consts": consts,
        "woff": woff.reshape(P, TAPS, CB), "grid": grid.reshape(CB, PIX), "w2": w2.reshape(P, TAPS * CB),
        "w3": w3.reshape(P, HALVES, C), "wq": wq.reshape(P, Q_COLS),
    }
    nc = bacc.Bacc("TRN2", target_bir_lowering=False, num_devices=1)
    args = [nc.dram_tensor(k, v.shape, F32, kind="ExternalInput").ap() for k, v in arrays.items()]
    out = nc.dram_tensor("out", (B, C, N), F32, kind="ExternalOutput").ap()
    build(nc, *args, out)
    r = run(nc, [arrays], core_ids=[0])
    return r.results[0]["out"].reshape(B, C, H, W)
```
